# Optimizing a Trainium2 kernel written in Bass

```python
import numpy as np
import jax
import jax.numpy as jnp

def _softmax(x, axis=-1):
    return jax.nn.softmax(x, axis=axis)

def _gelu(x):
    return jax.nn.gelu(x, approximate=True)

def _silu(x):
    return jax.nn.silu(x)

def _sigmoid(x):
    return jax.nn.sigmoid(x)

def _layernorm(x, axis=-1, eps=1e-05):
    m = jnp.mean(x, axis=axis, keepdims=True)
    v = jnp.var(x, axis=axis, keepdims=True)
    return (x - m) / jnp.sqrt(v + eps)

def _scatter_add(tgt, idx, src, axis=0):
    return tgt.at[idx].add(src)

def _segment_sum(src, seg, n):
    return jax.ops.segment_sum(src, seg, n)
kernel_name = 'mk_adaln_d1_jaxref_r4_6dfda8'

def setup_inputs(seed: int=0):
    np.random.seed(seed)
    _w = jnp.asarray

    def _L0_attn_setup():
        import jax, jax.numpy as jnp
        import numpy as np
        N_HEADS = 16
        EMBED = 256
        HEAD = EMBED // N_HEADS
        key = jax.random.key(seed)
        k1, k2, k3, k4, k5 = jax.random.split(key, 5)
        x = jax.random.normal(k1, (2, 512, EMBED), dtype=jnp.float32)
        s_in = 1.0 / np.sqrt(EMBED)
        W_qkv = jax.random.uniform(k2, (3 * EMBED, EMBED), minval=-s_in, maxval=s_in, dtype=jnp.float32)
        b_qkv = jax.random.uniform(k3, (3 * EMBED,), minval=-s_in, maxval=s_in, dtype=jnp.float32)
        W_out = jax.random.uniform(k4, (EMBED, EMBED), minval=-s_in, maxval=s_in, dtype=jnp.float32)
        b_out = jax.random.uniform(k5, (EMBED,), minval=-s_in, maxval=s_in, dtype=jnp.float32)
        return {'x': x, 'W_qkv': W_qkv, 'b_qkv': b_qkv, 'W_out': W_out, 'b_out': b_out}
    _L0_attn_in = _L0_attn_setup()

    def _L0_ffn_setup():
        import jax, jax.numpy as jnp
        import numpy as np
        B, S, D, H = (8, 256, 256, 1024)
        E, R = (3, 8)
        SCALING = 1.0 / R

        def _mole(x, W, b, A, Bm, Rw):
            gates = jax.nn.softmax(jnp.einsum('bsd,de->bse', x, Rw), axis=-1)
            base = jnp.einsum('bsd,dh->bsh', x, W) + b
            z = jnp.einsum('bsd,edr->ebsr', x, A)
            zg = z * jnp.transpose(gates, (2, 0, 1))[..., None]
            lora = jnp.einsum('ebsr,erh->bsh', zg, Bm)
            return base + SCALING * lora
        key = jax.random.key(seed)
        ks = jax.random.split(key, 12)
        s = lambda k, shape, scale: jax.random.normal(k, shape, dtype=jnp.float32) * scale
        return {'x': s(ks[0], (B, S, D), 1.0), 'W1': s(ks[1], (D, H), D ** (-0.5)), 'b1': jnp.zeros((H,), jnp.float32), 'A1': s(ks[2], (E, D, R), D ** (-0.5)), 'B1': s(ks[3], (E, R, H), 0.0) + s(ks[4], (E, R, H), R ** (-0.5)), 'R1': s(ks[5], (D, E), D ** (-0.5)), 'W2': s(ks[6], (H, D), H ** (-0.5)), 'b2': jnp.zeros((D,), jnp.float32), 'A2': s(ks[7], (E, H, R), H ** (-0.5)), 'B2': s(ks[8], (E, R, D), R ** (-0.5)), 'R2': s(ks[9], (H, E), H ** (-0.5))}
    _L0_ffn_in = _L0_ffn_setup()
    _L0_c = _w((lambda *s: np.random.randn(*s).astype(np.float32) * 0.05)(2, 256))
    _L0_wmod = _w((lambda *s: np.random.randn(*s).astype(np.float32) * 0.05)(256, 6 * 256) * 256 ** (-0.5))
    _d = {'L0_attn_x': _L0_attn_in['x'], 'L0_attn_W_qkv': _L0_attn_in['W_qkv'], 'L0_attn_b_qkv': _L0_attn_in['b_qkv'], 'L0_attn_W_out': _L0_attn_in['W_out'], 'L0_attn_b_out': _L0_attn_in['b_out'], 'L0_ffn_W1': _L0_ffn_in['W1'], 'L0_ffn_b1': _L0_ffn_in['b1'], 'L0_ffn_A1': _L0_ffn_in['A1'], 'L0_ffn_B1': _L0_ffn_in['B1'], 'L0_ffn_R1': _L0_ffn_in['R1'], 'L0_ffn_W2': _L0_ffn_in['W2'], 'L0_ffn_b2': _L0_ffn_in['b2'], 'L0_ffn_A2': _L0_ffn_in['A2'], 'L0_ffn_B2': _L0_ffn_in['B2'], 'L0_ffn_R2': _L0_ffn_in['R2'], 'L0_c': _L0_c, 'L0_wmod': _L0_wmod}
    _x0 = _d['L0_attn_x']
    _d['L0_attn_x'] = jax.random.normal(jax.random.fold_in(jax.random.key(seed), 1), (2, 2048, 256), dtype=_x0.dtype)
    del _x0
    return _d

def reference(L0_attn_x, L0_attn_W_qkv, L0_attn_b_qkv, L0_attn_W_out, L0_attn_b_out, L0_ffn_W1, L0_ffn_b1, L0_ffn_A1, L0_ffn_B1, L0_ffn_R1, L0_ffn_W2, L0_ffn_b2, L0_ffn_A2, L0_ffn_B2, L0_ffn_R2, L0_c, L0_wmod):

    def _L0_attn_ref(x, W_qkv, b_qkv, W_out, b_out):
        import jax, jax.numpy as jnp
        import numpy as np
        N_HEADS = 16
        EMBED = 256
        HEAD = EMBED // N_HEADS
        n, seq_len, _ = x.shape
        qkv = x @ W_qkv.T + b_qkv
        q, k, v = jnp.split(qkv, 3, axis=2)

        def heads(t):
            return t.reshape(n, seq_len, N_HEADS, HEAD).transpose(0, 2, 1, 3)
        q, k, v = (heads(q), heads(k), heads(v))
        logits = jnp.einsum('bhqd,bhkd->bhqk', q, k) / jnp.sqrt(jnp.float32(HEAD))
        causal = jnp.tril(jnp.ones((seq_len, seq_len), dtype=bool))
        logits = jnp.where(causal[None, None], logits, -jnp.inf)
        attn = jax.nn.softmax(logits, axis=-1)
        o = jnp.einsum('bhqk,bhkd->bhqd', attn, v)
        o = o.transpose(0, 2, 1, 3).reshape(n, seq_len, EMBED)
        return o @ W_out.T + b_out

    def _L0_ffn_ref(x, W1, b1, A1, B1, R1, W2, b2, A2, B2, R2):
        import jax, jax.numpy as jnp
        import numpy as np
        B, S, D, H = (8, 256, 256, 1024)
        E, R = (3, 8)
        SCALING = 1.0 / R

        def _mole(x, W, b, A, Bm, Rw):
            gates = jax.nn.softmax(jnp.einsum('bsd,de->bse', x, Rw), axis=-1)
            base = jnp.einsum('bsd,dh->bsh', x, W) + b
            z = jnp.einsum('bsd,edr->ebsr', x, A)
            zg = z * jnp.transpose(gates, (2, 0, 1))[..., None]
            lora = jnp.einsum('ebsr,erh->bsh', zg, Bm)
            return base + SCALING * lora
        h = _mole(x, W1, b1, A1, B1, R1)
        h = jax.nn.relu(h)
        return _mole(h, W2, b2, A2, B2, R2)
    x = L0_attn_x
    mod = (_silu(L0_c) @ L0_wmod).reshape(L0_c.shape[0], 6, 1, -1)
    sa, ca, ga, sb, cb, gb = (mod[:, 0], mod[:, 1], mod[:, 2], mod[:, 3], mod[:, 4], mod[:, 5])
    ga = (2 * (ga >= 0) - 1) * jnp.maximum(jnp.abs(ga), 0.25)
    gb = (2 * (gb >= 0) - 1) * jnp.maximum(jnp.abs(gb), 0.25)
    h = _layernorm(x, axis=-1) * (1 + ca) + sa
    x = x + ga * _L0_attn_ref(h, L0_attn_W_qkv, L0_attn_b_qkv, L0_attn_W_out, L0_attn_b_out)
    h = _layernorm(x, axis=-1) * (1 + cb) + sb
    x = x + gb * _L0_ffn_ref(h, L0_ffn_W1, L0_ffn_b1, L0_ffn_A1, L0_ffn_B1, L0_ffn_R1, L0_ffn_W2, L0_ffn_b2, L0_ffn_A2, L0_ffn_B2, L0_ffn_R2)
    return x

_drawn_inputs = setup_inputs


def setup_inputs(seed=0):
    import zlib

    import numpy as np

    out = dict(_drawn_inputs(seed))
    spreads = {'L0_ffn_b1': (0.0, 0.469), 'L0_ffn_b2': (0.0, 1.518)}
    factors = {'L0_attn_W_qkv': 8.0,
     'L0_attn_b_qkv': 8.0,
     'L0_attn_W_out': 6.946,
     'L0_attn_b_out': 27.97,
     'L0_ffn_A1': 3.677,
     'L0_ffn_B1': 3.716,
     'L0_ffn_R1': 7.047,
     'L0_ffn_A2': 3.802,
     'L0_ffn_B2': 3.921,
     'L0_ffn_R2': 6.618}
    for name, (base, spread) in spreads.items():
        noise = np.random.default_rng([zlib.crc32(name.encode()), seed]).standard_normal(out[name].shape)
        drawn = base * np.exp(spread * noise) if base else spread * noise
        out[name] = jnp.asarray(drawn.astype(out[name].dtype))
    for name, factor in factors.items():
        out[name] = (out[name] * factor).astype(out[name].dtype)
    return out
```

```python
from contextlib import ExitStack

import concourse.bass as bass
from concourse import mybir

P = 128
F32 = mybir.dt.float32
BF16 = mybir.dt.bfloat16
ALU = mybir.AluOpType
ACT = mybir.ActivationFunctionType
AX = mybir.AxisListType.X

B, S, D = 2, 2048, 256
NH, HD = 16, 16
FF = 1024
E, R = 3, 8
ER = E * R
ZC = ER + E
KC, FC = D // P, FF // P
T = B * S
BLK = 512
TT = BLK // P
NPAIR = S // BLK // 2
EPS = 1e-5
NEG = -3.0e38
GH = 4
NG = B * NH // GH
NPART = 3
PR = NPART * HD
QK_ROWS = 6 * HD
ST_ROWS = QK_ROWS + NPART
NJ = S // BLK
KT = [(J, t) for J in range(NJ) for t in range(4 * (J + 1))]
NKT = len(KT)
ST_BUFS, P_BUFS = 2, 4
LAST_OF_J = {n: KT[n][0] for n in range(NKT) if n + 1 == NKT or KT[n + 1][0] != KT[n][0]}
FIRST_OF_J = {n: KT[n][0] for n in range(NKT) if KT[n][1] == 0}


def max_units():
    units = []
    for J in range(NJ):
        for r in range(4):
            i = 4 * J + r
            for h in range(GH):
                for c in range(J):
                    units.append((J, i, h, 1, c, BLK, False))
            together = {0: 4, 1: 2, 2: 1, 3: 1}[r]
            for h in range(0, GH, together):
                units.append((J, i, h, together, J, (r + 1) * P, True))
    return units


MU = max_units()
NMU = len(MU)
LAST_MU = {w: MU[w][0] for w in range(NMU) if w + 1 == NMU or MU[w + 1][0] != MU[w][0]}
T_LAG, COPY_LAG = 3, 5


def tensor_slots():
    events = []
    for w in range(NMU):
        events.append(("mm", w))
        if w - T_LAG in LAST_MU:
            events.append(("tr", LAST_MU[w - T_LAG]))
    events.append(("tr", NJ - 1))
    slots, done = [], 0
    for u in range(2 * NKT):
        want = min(len(events), max(0, (u - 1) * len(events) // (2 * NKT - 5)))
        slots.append(events[done:want])
        done = max(done, want)
    slots[-1] = slots[-1] + events[done:]
    return slots


SLOTS = tensor_slots()


def alone(eng):
    eng.nop(nofuse=True)


def build_program(nc, x, cT, wmod, wqkvT, bqkv, bv, woutT, bout, w1, b1, ar1, bl1, w2, b2, ar2, bl2, out):
    qk_parts = nc.dram_tensor("qk_parts", [2, NH, PR, T], BF16, kind="Internal").ap()
    o_rows = nc.dram_tensor("o_rows", [NH, HD, T], F32, kind="Internal").ap()
    rden_rows = nc.dram_tensor("rden_rows", [NH, T], F32, kind="Internal").ap()

    with ExitStack() as whole:
        def sb(ctx, name, shape, dt=F32):
            return ctx.enter_context(nc.sbuf_tensor(name, shape, dt))

        def sem(name):
            return whole.enter_context(nc.semaphore(name))

        ps = whole.enter_context(nc.psum_tensor("ps", [P, 8, BLK], F32))
        w1_sb = sb(whole, "w1_sb", [P, KC, FF])
        ar1_sb = sb(whole, "ar1_sb", [P, KC, ZC])
        bl1_sb = sb(whole, "bl1_sb", [ER, FF])
        b1_sb = sb(whole, "b1_sb", [P, FC])
        woutg = sb(whole, "woutg", [P, B, KC, D])
        boutg = sb(whole, "boutg", [P, B, D])
        w2g = sb(whole, "w2g", [P, B, FC, D + ZC])
        bl2g = sb(whole, "bl2g", [ER, B, D])
        b2g = sb(whole, "b2g", [P, B, D])
        mod = sb(whole, "mod", [P, B, 4, KC])
        ident = sb(whole, "ident", [P, P])
        ident_bf = sb(whole, "ident_bf", [P, P], BF16)
        mask_q = sb(whole, "mask_q", [P, P], BF16)
        mask_k = sb(whole, "mask_k", [P, P], BF16)

        v_scope = whole.enter_context(ExitStack())
        v_nat = sb(v_scope, "v_nat", [P, T // P, D])
        proj = ExitStack()
        wqkv_sb = sb(proj, "wqkv_sb", [P, KC, 3 * D])
        bq_sb = sb(proj, "bq_sb", [P, 2 * KC])
        bv_sb = sb(proj, "bv_sb", [P, D])

        w_loaded = sem("w_loaded")
        cols_done, rows_done = sem("cols_done"), sem("rows_done")
        exp_c, dve0, pool0, act0 = sem("exp_c"), sem("dve0"), sem("pool0"), sem("act0")
        with ExitStack() as tmp, nc.Block() as block:
            c_sb = sb(tmp, "c_sb", [P, KC, B])
            ec = sb(tmp, "ec", [P, KC, B])
            silu = sb(tmp, "silu", [P, KC, B])
            silu_wide = sb(tmp, "silu_wide", [P, KC, B, P])
            ones = sb(tmp, "ones", [P, P])
            zeros = sb(tmp, "zeros", [P, P])
            wmod_sb = sb(tmp, "wmod_sb", [P, KC, 6 * D])
            w2_sb = sb(tmp, "w2_sb", [P, FC, D])
            wout_sb = sb(tmp, "wout_sb", [P, KC, D])
            bl2_sb = sb(tmp, "bl2_sb", [ER, D])
            bout_sb = sb(tmp, "bout_sb", [P, D])
            b2_sb = sb(tmp, "b2_sb", [P, D])
            gate = sb(tmp, "gate", [P, 2, B, D])
            gsign = sb(tmp, "gsign", [P, 2, B, D])
            gabs = sb(tmp, "gabs", [P, 2, B, D])
            loads = [
                (c_sb[:], cT.rearrange("(k p) b -> p k b", p=P)),
                (wmod_sb[:], wmod.rearrange("(k p) n -> p k n", p=P)),
                (wqkv_sb[:], wqkvT.rearrange("(k p) n -> p k n", p=P)),
                (bq_sb[:], bqkv), (bv_sb[:], bv.broadcast_to((P, D))),
                (wout_sb[:], woutT.rearrange("(k p) n -> p k n", p=P)),
                (bout_sb[:], bout.broadcast_to((P, D))),
                (w1_sb[:], w1.rearrange("(k p) n -> p k n", p=P)), (b1_sb[:], b1),
                (ar1_sb[:], ar1.rearrange("(k p) n -> p k n", p=P)), (bl1_sb[:], bl1),
                (w2_sb[:], w2.rearrange("(k p) n -> p k n", p=P)),
                (b2_sb[:], b2.broadcast_to((P, D))), (bl2_sb[:], bl2),
                (w2g[:, 0, :, D:], ar2.rearrange("(k p) n -> p k n", p=P)),
                (w2g[:, 1, :, D:], ar2.rearrange("(k p) n -> p k n", p=P)),
            ]

            @block.sync
            def _(sp):
                for dst, src in loads:
                    sp.dma_start(dst, src).then_inc(w_loaded, 16)

            @block.gpsimd
            def _(pool):
                pool.memset(ones[:], 1.0).then_inc(pool0, 1)
                pool.memset(zeros[:], 0.0).then_inc(pool0, 1)
                pool.wait_ge(pool0, 2)
                for dst in (ident, ident_bf):
                    pool.affine_select(out=dst[:], in_=ones[:], compare_op=ALU.is_equal, fill=0.0, base=0,
                                       pattern=[[-1, P]], channel_multiplier=1).then_inc(pool0, 1)
                pool.affine_select(out=mask_q[:], in_=zeros[:], compare_op=ALU.is_ge, fill=NEG, base=0,
                                   pattern=[[-1, P]], channel_multiplier=1).then_inc(pool0, 1)
                pool.affine_select(out=mask_k[:], in_=zeros[:], compare_op=ALU.is_ge, fill=NEG, base=0,
                                   pattern=[[1, P]], channel_multiplier=-1).then_inc(pool0, 1)

            @block.scalar
            def _(act):
                act.wait_ge(w_loaded, 16 * len(loads))
                act.activation(ec[:], c_sb[:], ACT.Exp, scale=-1.0).then_inc(exp_c, 1)

            @block.tensor
            def _(pe):
                pe.wait_ge(dve0, 3)
                for v, i in enumerate((1, 0, 4, 3)):
                    for m in range(KC):
                        for k in range(KC):
                            col = i * D + m * P
                            last = pe.matmul(ps[:, 0, (v * KC + m) * B:(v * KC + m + 1) * B],
                                             wmod_sb[:, k, col:col + P], silu[:, k, :],
                                             start=(k == 0), stop=(k == KC - 1))
                last.then_inc(cols_done, 1)
                pe.wait_ge(dve0, 3 + KC * B)
                for v, i in enumerate((2, 5)):
                    for b in range(B):
                        for k in range(KC):
                            last = pe.matmul(ps[:, 1 + v, b * D:(b + 1) * D], silu_wide[:, k, b, :],
                                             wmod_sb[:, k, i * D:(i + 1) * D],
                                             start=(k == 0), stop=(k == KC - 1))
                last.then_inc(rows_done, 1)

            @block.vector
            def _(dve):
                count = [0]

                def link(ins):
                    count[0] += 1
                    ins.then_inc(dve0, 1)
                    dve.wait_ge(dve0, count[0])

                dve.wait_ge(exp_c, 1)
                link(dve.tensor_scalar(ec[:], ec[:], 1.0, None, ALU.add))
                link(dve.reciprocal(ec[:], ec[:]))
                link(dve.tensor_tensor(silu[:], c_sb[:], ec[:], ALU.mult))
                dve.wait_ge(pool0, 2)
                for k in range(KC):
                    for b in range(B):
                        link(dve.tensor_scalar(silu_wide[:, k, b, :], ones[:], silu[:, k, b:b + 1], None,
                                               ALU.mult))
                link(dve.tensor_scalar(bq_sb[:, 0:KC], bq_sb[:, 0:KC], HD ** -0.5, None, ALU.mult))
                dve.wait_ge(cols_done, 1)
                cols = ps[:, 0, 0:4 * KC * B].rearrange("p (v m b) -> p v m b", v=4, m=KC)
                for v in range(4):
                    link(dve.tensor_scalar(mod[:, :, v, :].rearrange("p b m -> p m b"), cols[:, v],
                                           1.0 - v % 2, None, ALU.add))
                dve.wait_ge(rows_done, 1)
                for v in range(2):
                    link(dve.tensor_copy(gate[:, v].rearrange("p b d -> p (b d)"), ps[:, 1 + v, :]))
                link(dve.tensor_scalar(gsign[:], gate[:], 0.0, 2.0, ALU.is_ge, ALU.mult))
                gate_f, gsign_f, gabs_f = (t[:].rearrange("p v b d -> p (v b d)") for t in (gate, gsign, gabs))
                link(dve.scalar_tensor_tensor(out=gabs_f, in0=gate_f, scalar=-1.0, in1=gate_f,
                                              op0=ALU.mult, op1=ALU.max))
                link(dve.tensor_scalar(gabs_f, gabs_f, 0.25, None, ALU.max))
                link(dve.scalar_tensor_tensor(out=gate_f, in0=gsign_f, scalar=-1.0, in1=gabs_f,
                                              op0=ALU.add, op1=ALU.mult))
                for b in range(B):
                    for k in range(KC):
                        link(dve.tensor_tensor(woutg[:, b, k], wout_sb[:, k], gate[:, 0, b], ALU.mult))
                    for k in range(FC):
                        link(dve.tensor_tensor(w2g[:, b, k, 0:D], w2_sb[:, k], gate[:, 1, b], ALU.mult))
                    link(dve.tensor_tensor(boutg[:, b], bout_sb[:], gate[:, 0, b], ALU.mult))
                    link(dve.tensor_tensor(b2g[:, b], b2_sb[:], gate[:, 1, b], ALU.mult))
                    link(dve.tensor_tensor(bl2g[:, b], bl2_sb[:], gate[0:ER, 1, b], ALU.mult))

        x_in = [sem(f"x_in{q}") for q in range(2)]
        var_done, std_done, xhat_done, xT_done, h_done = (
            sem(n) for n in ("var_done", "std_done", "xhat_done", "xT_done", "h_done"))
        qk_done, v_done, qk_out, v_out = sem("qk_done"), sem("v_done"), sem("qk_out"), sem("v_out")
        part1_done, part2_done, rest1_done, part3_done = (
            sem(n) for n in ("part1_done", "part2_done", "rest1_done", "part3_done"))
        parts_stored = [sem(f"parts_stored{q}") for q in range(2)]
        dve1 = sem("dve1")
        xb_in = x.rearrange("(n t p) d -> n p t d", t=TT, p=P)

        def layer_norm(dve, link, it, q, xs, stats, mv, rstd, xhat, var_done, std_done, xhat_done):
            for t in range(TT):
                last = dve.bn_stats(stats[:, t, :], xs[:, t, :])
                link(last, wait=(t == TT - 1))
            alone(dve)
            for t in range(TT - 1):
                link(dve.bn_aggr(mv[:, t, :], stats[:, t, :]), wait=False)
            dve.bn_aggr(mv[:, TT - 1, :], stats[:, TT - 1, :]).then_inc(var_done, 1)
            dve.wait_ge(std_done, it * 2 + q + 1)
            link(dve.reciprocal(rstd[:], rstd[:]))
            for t in range(TT):
                last = dve.tensor_scalar(xhat[:, t, :], xs[:, t, :], mv[:, t, 0:1], rstd[:, t:t + 1],
                                         ALU.subtract, ALU.mult)
                if t < TT - 1:
                    link(last, wait=False)
            last.then_inc(xhat_done, 1)

        with ExitStack() as tmp, nc.Block() as block:
            xs = sb(tmp, "xs", [P, 2, TT, D])
            stats = sb(tmp, "stats", [P, 2, TT, 6])
            mv = sb(tmp, "mv", [P, 2, TT, 2])
            rstd = sb(tmp, "rstd", [P, 2, TT])
            eps = sb(tmp, "eps", [P, 1])
            xhat = sb(tmp, "xhat", [P, 2, TT, D])
            hT = sb(tmp, "hT", [P, 2, KC, BLK])
            qkf = sb(tmp, "qkf", [P, 2, 2 * KC, BLK])
            rest = sb(tmp, "rest", [P, 2, 2 * KC, BLK])
            parts = sb(tmp, "parts", [P, 2, NPART, 2 * KC, BLK], BF16)
            eps_set = sem("eps_set")

            @block.sync
            def _(sp):
                with sp.Fori(0, B) as b:
                    with sp.Fori(0, NPAIR) as pr:
                        it = b * NPAIR + pr
                        for q in range(2):
                            sp.wait_ge(xhat_done, it * 2)
                            sp.dma_start(xs[:, q], xb_in[it * 2 + q]).then_inc(x_in[q], 16)
                        for q in range(2):
                            sp.wait_ge(part1_done, it * 2 + q + 1)
                            sp.wait_ge(part2_done, it * 2 + q + 1)
                            sp.wait_ge(part3_done, it * 2 + q + 1)
                            for c in range(2 * KC):
                                for a in range(NPART):
                                    dst = qk_parts[c // KC, (c % KC) * 8:(c % KC) * 8 + 8,
                                                   a * HD:(a + 1) * HD,
                                                   bass.ds(it * (2 * BLK) + q * BLK, BLK)]
                                    sp.dma_start(dst, parts[:, q, a, c, :]).then_inc(parts_stored[q], 16)
                for q in range(2):
                    sp.wait_ge(parts_stored[q], 16 * NPART * 2 * KC * B * NPAIR)

            @block.tensor
            def _(pe):
                with pe.Fori(0, B) as b:
                    with pe.Fori(0, NPAIR) as pr:
                        it = b * NPAIR + pr
                        for q in range(2):
                            pe.wait_ge(xhat_done, it * 2 + q + 1)
                            pe.wait_ge(v_out, it * 2)
                            for k in range(KC):
                                for t in range(TT):
                                    last = pe.transpose(ps[:, 2 * q + k, t * P:(t + 1) * P],
                                                        xhat[:, q, t, k * P:(k + 1) * P], ident[:])
                                last.then_inc(xT_done, 1)
                        for q in range(2):
                            pe.wait_ge(h_done, (it * 2 + q + 1) * KC)
                            for c in range(2 * KC):
                                if q == 0:
                                    pe.wait_ge(qk_out, it * 4 * 2 * KC // 2)
                                else:
                                    pe.wait_ge(qk_out, it * 4 * KC + c + 1)
                                for k in range(KC):
                                    last = pe.matmul(ps[:, 4 + c, :], wqkv_sb[:, k, c * P:(c + 1) * P],
                                                     hT[:, q, k, :], start=(k == 0), stop=(k == KC - 1))
                                last.then_inc(qk_done, 1)
                            for t in range(TT):
                                for k in range(KC):
                                    last = pe.matmul(ps[:, 2 * q + t // 2, t % 2 * D:(t % 2 + 1) * D],
                                                     hT[:, q, k, t * P:(t + 1) * P],
                                                     wqkv_sb[:, k, 2 * D:], start=(k == 0),
                                                     stop=(k == KC - 1))
                            last.then_inc(v_done, 1)

            @block.scalar
            def _(act):
                act.wait_ge(eps_set, 1)
                with act.Fori(0, B) as b:
                    with act.Fori(0, NPAIR) as pr:
                        it = b * NPAIR + pr
                        for q in range(2):
                            act.wait_ge(var_done, it * 2 + q + 1)
                            act.activation(rstd[:, q], mv[:, q, :, 1], ACT.Sqrt, bias=eps[:]).then_inc(std_done, 1)
                        for q in range(2):
                            for k in range(KC):
                                act.wait_ge(xT_done, (it * 2 + q) * KC + k + 1)
                                act.wait_ge(v_done, it * 2)
                                alone(act)
                                act.activation(hT[:, q, k, :], ps[:, 2 * q + k, :], ACT.Identity,
                                               bias=mod[:, bass.ds(b, 1), 1, k].rearrange("p o -> p o"),
                                               scale=mod[:, bass.ds(b, 1), 0, k]).then_inc(h_done, 1)
                        for q in range(2):
                            act.wait_ge(rest1_done, it * 2)
                            act.wait_ge(part1_done, it * 2)
                            for c in range(2 * KC):
                                act.wait_ge(qk_done, (it * 2 + q) * 2 * KC + c + 1)
                                act.activation(qkf[:, q, c, :], ps[:, 4 + c, :], ACT.Identity,
                                               bias=bq_sb[:, c:c + 1],
                                               scale=(HD ** -0.5 if c < KC else 1.0)).then_inc(qk_out, 1)

            @block.gpsimd
            def _(pool):
                with pool.Fori(0, B) as b:
                    with pool.Fori(0, NPAIR) as pr:
                        it = b * NPAIR + pr
                        for q in range(2):
                            pool.wait_ge(qk_out, (it * 2 + q + 1) * 2 * KC)
                            pool.wait_ge(parts_stored[q], it * 16 * NPART * 2 * KC)
                            alone(pool)
                            pool.tensor_copy(parts[:, q, 0], qkf[:, q]).then_inc(part1_done, 1)
                            pool.wait_ge(rest1_done, it * 2 + q + 1)
                            alone(pool)
                            pool.tensor_copy(parts[:, q, 1], rest[:, q]).then_inc(part2_done, 1)

            @block.vector
            def _(dve):
                dve.memset(eps[:], EPS).then_inc(eps_set, 1)
                per_it = 2 * (TT + TT - 1 + 1 + TT - 1)
                with dve.Fori(0, B) as b:
                    with dve.Fori(0, NPAIR) as pr:
                        it = b * NPAIR + pr
                        count = [0]

                        def link(ins, wait=True):
                            count[0] += 1
                            ins.then_inc(dve1, 1)
                            if wait:
                                dve.wait_ge(dve1, it * per_it + count[0])

                        for q in range(2):
                            dve.wait_ge(x_in[q], (it + 1) * 16)
                            dve.wait_ge(xT_done, it * 2 * KC)
                            layer_norm(dve, link, it, q, xs[:, q], stats[:, q], mv[:, q], rstd[:, q],
                                       xhat[:, q], var_done, std_done, xhat_done)
                        for q in range(2):
                            dve.wait_ge(v_done, it * 2 + q + 1)
                            dve.tensor_tensor(
                                v_nat[:, bass.ds(it * (2 * TT) + q * TT, TT), :],
                                ps[:, 2 * q:2 * q + 2, :].rearrange("p a (t d) -> p (a t) d", t=2),
                                bv_sb[:].unsqueeze(1).broadcast_to((P, TT, D)), ALU.add).then_inc(v_out, 1)
                            dve.wait_ge(part1_done, it * 2 + q + 1)
                            dve.wait_ge(part2_done, it * 2)
                            dve.tensor_tensor(rest[:, q], qkf[:, q], parts[:, q, 0],
                                              ALU.subtract).then_inc(rest1_done, 1)
                            dve.wait_ge(part2_done, it * 2 + q + 1)
                            dve.tensor_tensor(parts[:, q, 2], rest[:, q], parts[:, q, 1],
                                              ALU.subtract).then_inc(part3_done, 1)
                        assert count[0] == per_it
        proj.close()

        k_in, q_in, m_in = ([[sem(f"{n}_in{c}{J}") for J in range(NJ)] for c in range(2)] for n in "kqm")
        st_done, exp_done, pv_done, max_mm, max_red = (
            sem(n) for n in ("st_done", "exp_done", "pv_done", "max_mm", "max_red"))
        m_parts, m_turned, m_copied = sem("m_parts"), sem("m_turned"), sem("m_copied")
        o_out, v_wide, rden_done, ones_set = sem("o_out"), sem("v_wide"), sem("rden_done"), sem("ones_set")
        o_stored = [sem(f"o_stored{q}") for q in range(2)]
        den_in = [sem(f"den_in{q}") for q in range(2)]
        rden_stored, dve2 = sem("rden_stored"), sem("dve2")
        K_DMAS, Q_DMAS, O_DMAS = 3, 6, GH
        with ExitStack() as tmp, nc.Block() as block:
            kst = [sb(tmp, f"kst{q}", [P, NJ, GH, BLK], BF16) for q in range(2)]
            qst = [sb(tmp, f"qst{q}", [P, NJ, GH, BLK], BF16) for q in range(2)]
            vw = sb(tmp, "vw", [P, 2, S // P, GH, 2 * HD])
            prob = sb(tmp, "prob", [P, P_BUFS, GH, BLK])
            mx = sb(tmp, "mx", [P, GH, 4, NJ])
            negm = sb(tmp, "negm", [P, 2, GH * 4])
            mparts = sb(tmp, "mparts", [P, NPART, GH * 4], BF16)
            mT = sb(tmp, "mT", [NPART * GH * 4, NJ, P], BF16)
            o_sb = sb(tmp, "o_sb", [P, 2, BLK])
            den = sb(tmp, "den", [P, 2, 64])
            rden = sb(tmp, "rden", [P, 2, 64])
            S_BANK, O_BANK, M_BANK = 4, 6, 7

            def load_q(sp, g, hg, J):
                c = g % 2
                for row, a in enumerate((0, 0, 0, 1, 1, 2)):
                    src = qk_parts[0, bass.ds(hg * GH, GH), a * HD:(a + 1) * HD,
                                   c * S + J * BLK:c * S + (J + 1) * BLK].rearrange("h r t -> r h t")
                    sp.dma_start(qst[c][row * HD:(row + 1) * HD, J],
                                 src).then_inc(q_in[c][J], 16)

            def load_k(sp, g, hg, J):
                c = g % 2
                for row, n in ((0, 3), (3, 2), (5, 1)):
                    src = qk_parts[1, bass.ds(hg * GH, GH), 0:n * HD,
                                   c * S + J * BLK:c * S + (J + 1) * BLK].rearrange("h r t -> r h t")
                    sp.dma_start(kst[c][row * HD:(row + n) * HD, J],
                                 src).then_inc(k_in[c][J], 16)

            def sync_step(sp, s, c, hs, cur, nxt, far):
                nhs = hs + c
                nc_ = 1 - c
                for J in range(NJ):
                    if nxt:
                        sp.wait_ge(m_copied, (s + 1) * NJ + J + 1)
                        for a in range(NPART):
                            sp.dma_start(qst[nc_][QK_ROWS + a:QK_ROWS + a + 1, J],
                                         mT[a * 16:(a + 1) * 16, J, :]).then_inc(m_in[nc_][J], 16)
                    if cur and far:
                        sp.wait_ge(st_done, s * 2 * NKT + 2 * (1 + max(n for n in range(NKT) if KT[n][0] == J)))
                        load_q(sp, c, hs + 1, J)
                    if cur and far and J == NJ - 1:
                        for j in range(NJ):
                            load_k(sp, c, hs + 1, j)
                    if cur:
                        sp.wait_ge(o_out, s * NJ + J + 1)
                        cols = slice(c * S + J * BLK, c * S + (J + 1) * BLK)
                        for h in range(GH):
                            sp.dma_start(o_rows[bass.ds(hs * GH + h, 1), :, cols]
                                         .rearrange("o r t -> (o r) t"),
                                         o_sb[2 * HD * h:2 * HD * h + HD, J % 2, :]
                                         ).then_inc(o_stored[J % 2], 16)
                            sp.dma_start(den[32 * J + 8 * h:32 * J + 8 * h + 8, c, :],
                                         o_sb[2 * HD * h + HD:2 * HD * h + HD + 1, J % 2, :]
                                         ).then_inc(den_in[J % 2], 16)
                    if cur and J == 1 and not (isinstance(s, int) and s == 0):
                        store_rden(sp, s - 1, 1 - c, hs - 1 + c)

            def store_rden(sp, s, c, hs):
                sp.wait_ge(rden_done, s + 1)
                for J in range(NJ):
                    sp.dma_start(rden_rows[bass.ds(hs * GH, GH), c * S + J * BLK:c * S + (J + 1) * BLK],
                                 rden[32 * J:32 * J + 32, c, :]).then_inc(rden_stored, 16)

            def tensor_step(pe, s, c, hs, cur, nxt):
                g, q, k = s + 1, qst[1 - c], kst[1 - c]

                def max_mm_unit(w):
                    J, i, h0, nh, cb, width, diagonal = MU[w]
                    if w == 0 or MU[w - 1][0] != J:
                        pe.wait_ge(q_in[1 - c][J], loads(hs + c, Q_DMAS))
                        pe.wait_ge(k_in[1 - c][J], loads(hs + c, K_DMAS))
                    if not (isinstance(g, int) and g == 0 and w < 2):
                        pe.wait_ge(max_red, g * NMU + w - 1)
                    for h in range(nh):
                        at = ps[:, S_BANK + w % 2, h * width:(h + 1) * width]
                        last = pe.matmul(at, q[0:QK_ROWS, J, h0 + h, i % 4 * P:(i % 4 + 1) * P],
                                         k[0:QK_ROWS, cb, h0 + h, 0:width],
                                         start=True, stop=not diagonal)
                        if diagonal:
                            last = pe.matmul(at[:, width - P:width], ident_bf[:], mask_q[:],
                                             start=False, stop=True)
                    last.then_inc(max_mm, 1)

                def turn_maxima(J):
                    pe.wait_ge(m_parts, g * NJ + J + 1)
                    alone(pe)
                    pe.transpose(ps[0:NPART * 16, M_BANK, 0:P // 2].bitcast(BF16),
                                 mparts[:].rearrange("p a x -> p (a x)"), ident_bf[:]).then_inc(m_turned, 1)

                def maxima(slot):
                    for kind, n in SLOTS[slot]:
                        max_mm_unit(n) if kind == "mm" else turn_maxima(n)

                def logits(n, pair):
                    J, t = KT[n]
                    u = 2 * n + pair
                    skip = max(0, t - 4 * J) * P
                    width = BLK - skip
                    if n in FIRST_OF_J and pair == 0:
                        pe.wait_ge(m_in[c][J], loads(hs, NPART))
                    if not (isinstance(s, int) and s == 0 and u < 2):
                        pe.wait_ge(exp_done, s * 2 * NKT + u - 1)
                    for h in range(2 * pair, 2 * pair + 2):
                        last = pe.matmul(ps[:, h, 0:width], kst[c][0:ST_ROWS, t // 4, h, t % 4 * P:(t % 4 + 1) * P],
                                         qst[c][0:ST_ROWS, J, h, skip:BLK],
                                         start=True, stop=(t < 4 * J))
                        if t >= 4 * J:
                            last = pe.matmul(ps[:, h, 0:P], ident_bf[:], mask_k[:], start=False, stop=True)
                    last.then_inc(st_done, 1)

                def values(n):
                    J, t = KT[n]
                    skip = max(0, t - 4 * J) * P
                    pe.wait_ge(exp_done, s * 2 * NKT + 2 * n + 2)
                    if n == 0:
                        pe.wait_ge(v_wide, s + 1)
                    if n in FIRST_OF_J and not (isinstance(s, int) and s == 0 and J == 0):
                        pe.wait_ge(o_out, s * NJ + J)
                    for h in range(GH):
                        last = pe.matmul(ps[32 * h:32 * h + 32, O_BANK, skip:BLK], vw[:, c, t, h, :],
                                         prob[:, n % P_BUFS, h, 0:BLK - skip],
                                         start=(t == 0), stop=(n in LAST_OF_J), tile_position=(0, 32 * h))
                    last.then_inc(pv_done, 1)

                if not cur:
                    pe.wait_ge(ones_set, 2)
                    for slot in range(2 * NKT):
                        maxima(slot)
                    return
                for n in range(NKT):
                    for pair in range(2):
                        logits(n, pair)
                        if nxt:
                            maxima(2 * n + pair)
                    if n >= 1:
                        values(n - 1)
                values(NKT - 1)

            def scalar_step(act, s, c):
                def copy_out(J):
                    act.wait_ge(pv_done, s * NKT + 1 + max(n for n in range(NKT) if KT[n][0] == J))
                    if J >= 2:
                        act.wait_ge(o_stored[J % 2], s * 32 * O_DMAS + 16 * O_DMAS)
                        act.wait_ge(den_in[J % 2], s * 32 * O_DMAS + 16 * O_DMAS)
                    elif not (isinstance(s, int) and s == 0):
                        act.wait_ge(o_stored[J % 2], s * 32 * O_DMAS)
                        act.wait_ge(den_in[J % 2], s * 32 * O_DMAS)
                    act.copy(o_sb[:, J % 2, :], ps[:, O_BANK, :]).then_inc(o_out, 1)

                for n in range(NKT):
                    J, t = KT[n]
                    width = BLK - max(0, t - 4 * J) * P
                    if not (isinstance(s, int) and s == 0 and n < P_BUFS):
                        act.wait_ge(pv_done, s * NKT + n - P_BUFS + 1)
                    for pair in range(2):
                        act.wait_ge(st_done, s * 2 * NKT + 2 * n + pair + 1)
                        act.activation(prob[:, n % P_BUFS, 2 * pair:2 * pair + 2, 0:width],
                                       ps[:, 2 * pair:2 * pair + 2, 0:width], ACT.Exp).then_inc(exp_done, 1)
                    if n >= 1 and n - 1 in LAST_OF_J:
                        copy_out(LAST_OF_J[n - 1])
                copy_out(NJ - 1)

            def vector_step(dve, s, c, hs, cur, nxt):
                g = s + 1
                count = [0]
                per_s = 4 * NJ

                def link(ins):
                    count[0] += 1
                    ins.then_inc(dve2, 1)
                    dve.wait_ge(dve2, g * per_s + count[0])

                def make_parts(J):
                    m = negm[:, 0, :]
                    link(dve.tensor_reduce(m.rearrange("p (h i) -> p h i", i=4), mx[:, :, :, 0:J + 1],
                                           AX, ALU.max, negate=True))
                    if not (isinstance(g, int) and g == 0 and J == 0):
                        dve.wait_ge(m_turned, g * NJ + J)
                    link(dve.tensor_copy(mparts[:, 0, :], m))
                    link(dve.tensor_tensor(negm[:, 1, :], m, mparts[:, 0, :], ALU.subtract))
                    link(dve.tensor_copy(mparts[:, 1, :], negm[:, 1, :]))
                    dve.tensor_tensor(mparts[:, 2, :], negm[:, 1, :], mparts[:, 1, :],
                                      ALU.subtract).then_inc(m_parts, 1)

                def copy_parts(J):
                    dve.wait_ge(m_turned, g * NJ + J + 1)
                    if not (isinstance(g, int) and g == 0):
                        dve.wait_ge(m_in[c][J], loads(hs, NPART))
                    dve.tensor_copy(mT[:, J, :], ps[0:NPART * 16, M_BANK, 0:P // 2].bitcast(BF16)
                                    ).then_inc(m_copied, 1)

                if nxt:
                    for w in range(NMU):
                        J, i, h0, nh, cb, width, _ = MU[w]
                        dve.wait_ge(max_mm, g * NMU + w + 1)
                        dve.tensor_reduce(mx[:, h0:h0 + nh, i % 4, cb],
                                          ps[:, S_BANK + w % 2, 0:nh * width]
                                          .rearrange("p (h x) -> p h x", h=nh), AX, ALU.max).then_inc(max_red, 1)
                        if w in LAST_MU:
                            dve.wait_ge(max_red, g * NMU + w + 1)
                            make_parts(LAST_MU[w])
                        if w - COPY_LAG in LAST_MU:
                            copy_parts(LAST_MU[w - COPY_LAG])
                        if w == NMU // 2 and not (isinstance(s, int) and s <= 0):
                            invert(dve, s - 1, 1 - c)
                    copy_parts(NJ - 1)
                    assert count[0] == per_s

            def invert(dve, s, c):
                for q in range(2):
                    dve.wait_ge(den_in[q], (s + 1) * 32 * O_DMAS)
                dve.wait_ge(rden_stored, s * 16 * NJ)
                dve.reciprocal(rden[:, c, :], den[:, c, :]).then_inc(rden_done, 1)

            def loads(hs, dmas):
                return (hs + 1) * 16 * dmas

            def over_steps(eng, step):
                step(0, 0, 0, True)
                with eng.Fori(0, (NG - 2) // 2) as k:
                    step(k * 2 + 1, 1, k, True)
                    step(k * 2 + 2, 0, k + 1, True)
                step(NG - 1, 1, NG // 2 - 1, False)

            @block.sync
            def _(sp):
                for J in range(NJ):
                    load_q(sp, 0, 0, J)
                    load_k(sp, 0, 0, J)
                for J in range(NJ):
                    load_q(sp, 1, 0, J)
                    load_k(sp, 1, 0, J)
                sync_step(sp, -1, 1, -1, False, True, False)
                sync_step(sp, 0, 0, 0, True, True, True)
                with sp.Fori(0, (NG - 4) // 2) as k:
                    sync_step(sp, k * 2 + 1, 1, k, True, True, True)
                    sync_step(sp, k * 2 + 2, 0, k + 1, True, True, True)
                sync_step(sp, NG - 3, 1, NG // 2 - 2, True, True, True)
                sync_step(sp, NG - 2, 0, NG // 2 - 1, True, True, False)
                sync_step(sp, NG - 1, 1, NG // 2 - 1, True, False, False)
                store_rden(sp, NG - 1, 1, NG // 2 - 1)
                sp.wait_ge(rden_stored, 16 * NJ * NG)
                for q in range(2):
                    sp.wait_ge(o_stored[q], 16 * O_DMAS * NJ // 2 * NG)

            @block.tensor
            def _(pe):
                tensor_step(pe, -1, 1, -1, False, True)
                over_steps(pe, lambda s, c, hs, nxt: tensor_step(pe, s, c, hs, True, nxt))

            @block.scalar
            def _(act):
                over_steps(act, lambda s, c, hs, nxt: scalar_step(act, s, c))

            @block.vector
            def _(dve):
                vector_step(dve, -1, 1, -1, False, True)
                over_steps(dve, lambda s, c, hs, nxt: vector_step(dve, s, c, hs, True, nxt))
                invert(dve, NG - 2, 0)
                invert(dve, NG - 1, 1)

            @block.gpsimd
            def _(pool):
                for q in range(2):
                    pool.memset(kst[q][QK_ROWS:ST_ROWS], 1.0).then_inc(ones_set, 1)
                pool.wait_ge(ones_set, 2)
                pool.memset(vw[:, :, :, :, HD:].rearrange("p c t h d -> p (c t h) d"), 1.0).then_inc(pool0, 1)
                pool.wait_ge(pool0, 7)

                def widen(s, c, hs, nxt):
                    if not (isinstance(s, int) and s < 2):
                        pool.wait_ge(pv_done, (s - 1) * NKT)
                    nt = S // P
                    pool.tensor_copy(vw[:, c, :, :, 0:HD],
                                     v_nat[:, c * nt:(c + 1) * nt, bass.ds(hs * (GH * HD), GH * HD)]
                                     .rearrange("p t (h d) -> p t h d", d=HD)).then_inc(v_wide, 1)

                widen(0, 0, 0, True)
                widen(1, 1, 0, True)
                with pool.Fori(0, (NG - 2) // 2) as k:
                    widen(k * 2 + 2, 0, k + 1, True)
                    widen(k * 2 + 3, 1, k + 1, True)

        v_scope.close()

        names = ("o_norm", "p_done", "x1_done", "xbias_done", "x1b_done", "var2", "std2", "xhat2", "xT2",
                 "h2_done", "z1_done", "z1_sub", "z1_exp", "zg1_done", "zg1_turned", "zg1_copied",
                 "f1_done", "f1_out", "f2_done", "z2_sub", "z2_exp", "zg2_done", "zg2_turned",
                 "zg2_copied", "y_psum", "y_done", "dve3")
        (o_norm, p_done, x1_done, xbias_done, x1b_done, var2, std2, xhat2, xT2,
         h2_done, z1_done, z1_sub, z1_exp, zg1_done, zg1_turned, zg1_copied,
         f1_done, f1_out, f2_done, z2_sub, z2_exp, zg2_done, zg2_turned,
         zg2_copied, y_psum, y_done, dve3) = (sem("f_" + n) for n in names)
        o_in = [sem(f"o_in{q}") for q in range(2)]
        x2_in = [sem(f"x2_in{q}") for q in range(2)]
        y_stored = [sem(f"y_stored{q}") for q in range(2)]
        out_b = out.rearrange("(n t p) d -> n p t d", t=TT, p=P)
        o_feat = o_rows.rearrange("h r t -> (h r) t")
        with ExitStack() as tmp, nc.Block() as block:
            xs = sb(tmp, "xs2", [P, 2, TT, D])
            o_raw = sb(tmp, "o_raw", [P, 2, KC, BLK])
            rd = sb(tmp, "rd", [P, 2, KC, BLK])
            x1 = sb(tmp, "x1", [P, 2, TT, D])
            x1b = sb(tmp, "x1b", [P, 2, TT, D])
            y = sb(tmp, "y", [P, 2, TT, D])
            stats = sb(tmp, "stats2", [P, 2, TT, 6])
            mv = sb(tmp, "mv2", [P, 2, TT, 2])
            rstd = sb(tmp, "rstd2", [P, 2, TT])
            eps = sb(tmp, "eps2", [P, 1])
            xhat = sb(tmp, "xhat2", [P, 2, TT, D])
            hT = sb(tmp, "hT2", [P, 2, KC, BLK])
            hid = sb(tmp, "hid", [P, FC, BLK])
            gmax = sb(tmp, "gmax", [P, 2, TT])
            gexp = sb(tmp, "gexp", [P, 2, TT, E])
            gsum = sb(tmp, "gsum", [P, 2, TT])
            zg = sb(tmp, "zg", [P, 2, TT, ER])
            zgT = sb(tmp, "zgT", [ER, 2, BLK])
            T_BANK, H_BANK, Z_BANK, G_BANK = 2, 4, 6, 7

            def turn(pe, it, q, ready, turned, free, free_count):
                pe.wait_ge(ready, it * 2 + q + 1)
                pe.wait_ge(free, free_count)
                for t in range(TT):
                    last = pe.transpose(ps[0:ER, G_BANK, t * P:(t + 1) * P], zg[:, q, t, :], ident[:])
                last.then_inc(turned, 1)

            @block.sync
            def _(sp):
                with sp.Fori(0, B) as b:
                    with sp.Fori(0, NPAIR) as pr:
                        it = b * NPAIR + pr
                        for q in range(2):
                            n = it * 2 + q
                            sp.wait_ge(o_norm, it * 2)
                            for k in range(KC):
                                sp.dma_start(o_raw[:, q, k, :],
                                             o_feat[k * P:(k + 1) * P, bass.ds(n * BLK, BLK)]).then_inc(o_in[q], 16)
                                sp.dma_start(rd[:, q, k, :],
                                             rden_rows[k * 8:(k + 1) * 8, bass.ds(n * BLK, BLK)].unsqueeze(1)
                                             .broadcast_to((8, HD, BLK))).then_inc(o_in[q], 16)
                            sp.wait_ge(x1_done, it * 2)
                            sp.dma_start(xs[:, q], xb_in[n]).then_inc(x2_in[q], 16)
                        for q in range(2):
                            sp.wait_ge(y_done, it * 2 + q + 1)
                            sp.dma_start(out_b[it * 2 + q], y[:, q]).then_inc(y_stored[q], 16)
                for q in range(2):
                    sp.wait_ge(y_stored[q], 16 * B * NPAIR)

            @block.gpsimd
            def _(pool):
                with pool.Fori(0, B) as b:
                    with pool.Fori(0, NPAIR) as pr:
                        it = b * NPAIR + pr
                        for q in range(2):
                            pool.wait_ge(x2_in[q], (it + 1) * 16)
                            alone(pool)
                            pool.tensor_tensor(xs[:, q], xs[:, q],
                                               boutg[:, bass.ds(b, 1), :].broadcast_to((P, TT, D)),
                                               ALU.add).then_inc(xbias_done, 1)
                        for q in range(2):
                            pool.wait_ge(x1_done, it * 2 + q + 1)
                            pool.wait_ge(y_done, it * 2)
                            alone(pool)
                            pool.tensor_tensor(x1b[:, q], x1[:, q],
                                               b2g[:, bass.ds(b, 1), :].broadcast_to((P, TT, D)),
                                               ALU.add).then_inc(x1b_done, 1)

            @block.tensor
            def _(pe):
                with pe.Fori(0, B) as b:
                    with pe.Fori(0, NPAIR) as pr:
                        it = b * NPAIR + pr
                        for q in range(2):
                            pe.wait_ge(o_norm, it * 2 + q + 1)
                            pe.wait_ge(y_done, it * 2)
                            if q == 1:
                                pe.wait_ge(x1_done, it * 2 + 1)
                            for t in range(TT):
                                for k in range(KC):
                                    last = pe.matmul(ps[:, t // 2, t % 2 * D:(t % 2 + 1) * D],
                                                     o_raw[:, q, k, t * P:(t + 1) * P],
                                                     woutg[:, bass.ds(b, 1), k, :].rearrange("p o d -> p (o d)"),
                                                     start=(k == 0), stop=(k == KC - 1))
                            last.then_inc(p_done, 1)
                        for q in range(2):
                            pe.wait_ge(xhat2, it * 2 + q + 1)
                            if q == 1:
                                pe.wait_ge(h2_done, (it * 2 + 1) * KC)
                            for k in range(KC):
                                for t in range(TT):
                                    last = pe.transpose(ps[:, T_BANK + k, t * P:(t + 1) * P],
                                                        xhat[:, q, t, k * P:(k + 1) * P], ident[:])
                                last.then_inc(xT2, 1)
                        for q in range(2):
                            pe.wait_ge(h2_done, (it * 2 + q + 1) * KC)
                            if q == 1:
                                pe.wait_ge(zg1_done, it * 2 + 1)
                            for t in range(TT):
                                for k in range(KC):
                                    last = pe.matmul(ps[:, Z_BANK, t * 32:t * 32 + ZC],
                                                     hT[:, q, k, t * P:(t + 1) * P], ar1_sb[:, k, :],
                                                     start=(k == 0), stop=(k == KC - 1))
                            last.then_inc(z1_done, 1)
                        for q in range(2):
                            turn(pe, it, q, zg1_done, zg1_turned, zg2_copied if q == 0 else zg1_copied,
                                 it * 2 if q == 0 else it * 2 + 1)
                        for q in range(2):
                            pe.wait_ge(zg1_copied, it * 2 + q + 1)
                            for m in range(FC):
                                if m < 2:
                                    pe.wait_ge(f1_out, (it * 2 + q) * FC)
                                else:
                                    pe.wait_ge(f1_out, (it * 2 + q) * FC + m - 1)
                                for k in range(KC):
                                    pe.matmul(ps[:, H_BANK + m % 2, :], w1_sb[:, k, m * P:(m + 1) * P],
                                              hT[:, q, k, :], start=(k == 0), stop=False)
                                pe.matmul(ps[:, H_BANK + m % 2, :], bl1_sb[:, m * P:(m + 1) * P],
                                          zgT[:, q, :], start=False, stop=True).then_inc(f1_done, 1)
                            if q == 1:
                                pe.wait_ge(y_done, it * 2 + 1)
                            pe.wait_ge(f1_out, (it * 2 + q + 1) * FC)
                            for t in range(TT):
                                for m in range(FC):
                                    last = pe.matmul(ps[:, t, 0:D + ZC], hid[:, m, t * P:(t + 1) * P],
                                                     w2g[:, bass.ds(b, 1), m, :].rearrange("p o d -> p (o d)"),
                                                     start=(m == 0), stop=(m == FC - 1))
                            last.then_inc(f2_done, 1)
                            turn(pe, it, q, zg2_done, zg2_turned, zg2_copied if q else zg1_copied,
                                 it * 2 + 1 if q else it * 2 + 2)
                            pe.wait_ge(zg2_copied, it * 2 + q + 1)
                            alone(pe)
                            for t in range(TT):
                                last = pe.matmul(ps[:, t, 0:D], zgT[:, q, t * P:(t + 1) * P],
                                                 bl2g[:, bass.ds(b, 1), :].rearrange("p o d -> p (o d)"),
                                                 start=False, stop=True, skip_group_check=True)
                            last.then_inc(y_psum, 1)

            @block.scalar
            def _(act):
                with act.Fori(0, B) as b:
                    with act.Fori(0, NPAIR) as pr:
                        it = b * NPAIR + pr
                        for q in range(2):
                            act.wait_ge(var2, it * 2 + q + 1)
                            act.activation(rstd[:, q], mv[:, q, :, 1], ACT.Sqrt, bias=eps[:]).then_inc(std2, 1)
                        for q in range(2):
                            for k in range(KC):
                                act.wait_ge(xT2, (it * 2 + q) * KC + k + 1)
                                act.wait_ge(f1_done, it * 2 * FC)
                                alone(act)
                                act.activation(hT[:, q, k, :], ps[:, T_BANK + k, :], ACT.Identity,
                                               bias=mod[:, bass.ds(b, 1), 3, k],
                                               scale=mod[:, bass.ds(b, 1), 2, k]).then_inc(h2_done, 1)
                        for q in range(2):
                            act.wait_ge(z1_sub, it * 2 + q + 1)
                            act.activation(gexp[:, q], gexp[:, q], ACT.Exp).then_inc(z1_exp, 1)
                        for q in range(2):
                            act.wait_ge(zg1_turned, it * 2 + q + 1)
                            act.wait_ge(y_psum, it * 2)
                            act.copy(zgT[:, q, :], ps[0:ER, G_BANK, :]).then_inc(zg1_copied, 1)
                        for q in range(2):
                            act.wait_ge(f2_done, it * 2 + q)
                            for m in range(FC):
                                act.wait_ge(f1_done, (it * 2 + q) * FC + m + 1)
                                act.activation(hid[:, m, :], ps[:, H_BANK + m % 2, :], ACT.Relu,
                                               bias=b1_sb[:, m:m + 1]).then_inc(f1_out, 1)
                            act.wait_ge(z2_sub, it * 2 + q + 1)
                            act.activation(gexp[:, q], gexp[:, q], ACT.Exp).then_inc(z2_exp, 1)
                            act.wait_ge(zg2_turned, it * 2 + q + 1)
                            act.copy(zgT[:, q, :], ps[0:ER, G_BANK, :]).then_inc(zg2_copied, 1)

            @block.vector
            def _(dve):
                dve.memset(eps[:], EPS).then_inc(dve3, 1)
                per_it = 2 * (TT + TT - 1 + 1 + TT - 1) + 2 * 2 * 4 + 2
                with dve.Fori(0, B) as b:
                    with dve.Fori(0, NPAIR) as pr:
                        it = b * NPAIR + pr
                        count = [0]

                        def link(ins, wait=True):
                            count[0] += 1
                            ins.then_inc(dve3, 1)
                            if wait:
                                dve.wait_ge(dve3, it * per_it + count[0] + 1)

                        def route(q, zv, lv, sub, exp_done, zg_done):
                            link(dve.tensor_reduce(gmax[:, q], lv, AX, ALU.max))
                            dve.tensor_tensor(gexp[:, q], lv, gmax[:, q].unsqueeze(2).broadcast_to((P, TT, E)),
                                              ALU.subtract).then_inc(sub, 1)
                            dve.wait_ge(exp_done, it * 2 + q + 1)
                            link(dve.tensor_reduce(gsum[:, q], gexp[:, q], AX, ALU.add))
                            link(dve.reciprocal(gsum[:, q], gsum[:, q]))
                            link(dve.scalar_tensor_tensor(
                                out=gexp[:, q], in0=gexp[:, q], scalar=1.0 / R,
                                in1=gsum[:, q].unsqueeze(2).broadcast_to((P, TT, E)),
                                op0=ALU.mult, op1=ALU.mult))
                            dve.tensor_tensor(zg[:, q].rearrange("p t (e r) -> p t e r", r=R),
                                              zv.rearrange("p t (e r) -> p t e r", r=R),
                                              gexp[:, q].unsqueeze(3).broadcast_to((P, TT, E, R)),
                                              ALU.mult).then_inc(zg_done, 1)

                        for q in range(2):
                            dve.wait_ge(o_in[q], (it + 1) * 16 * 2 * KC)
                            dve.tensor_tensor(o_raw[:, q], o_raw[:, q], rd[:, q], ALU.mult).then_inc(o_norm, 1)
                        for q in range(2):
                            dve.wait_ge(p_done, it * 2 + q + 1)
                            dve.wait_ge(xbias_done, it * 2 + q + 1)
                            dve.wait_ge(x1b_done, it * 2)
                            dve.tensor_tensor(x1[:, q], ps[:, 0:2, :].rearrange("p a (t d) -> p (a t) d", t=2),
                                              xs[:, q], ALU.add).then_inc(x1_done, 1)
                            dve.wait_ge(x1_done, it * 2 + q + 1)
                            dve.wait_ge(xT2, it * 2 * KC)
                            layer_norm(dve, link, it, q, x1[:, q], stats[:, q], mv[:, q], rstd[:, q],
                                       xhat[:, q], var2, std2, xhat2)
                        z1 = ps[:, Z_BANK, 0:TT * 32].rearrange("p (t c) -> p t c", c=32)
                        for q in range(2):
                            dve.wait_ge(z1_done, it * 2 + q + 1)
                            route(q, z1[:, :, 0:ER], z1[:, :, ER:ZC], z1_sub, z1_exp, zg1_done)
                        for q in range(2):
                            dve.wait_ge(f2_done, it * 2 + q + 1)
                            route(q, ps[:, 0:TT, D:D + ER], ps[:, 0:TT, D + ER:D + ZC], z2_sub, z2_exp, zg2_done)
                            dve.wait_ge(y_psum, it * 2 + q + 1)
                            dve.wait_ge(x1b_done, it * 2 + q + 1)
                            dve.wait_ge(y_stored[q], it * 16)
                            dve.tensor_tensor(y[:, q], ps[:, 0:TT, 0:D], x1b[:, q], ALU.add).then_inc(y_done, 1)
                            link(dve.tensor_copy(gmax[:, q], gsum[:, q]), wait=False)
                        assert count[0] == per_it


_NAMES = ["x", "cT", "wmod", "wqkvT", "bqkv", "bv", "woutT", "bout", "w1", "b1", "ar1", "bl1", "w2", "b2",
          "ar2", "bl2"]


def kernel(**inputs):
    import numpy as np
    import concourse.bacc as bacc
    from concourse.bass_utils import run_bass_kernel_spmd

    a = {k.removeprefix("L0_"): np.asarray(v) for k, v in inputs.items()}
    laid = {
        "x": a["attn_x"].reshape(T, D), "cT": a["c"].T, "wmod": a["wmod"],
        "wqkvT": a["attn_W_qkv"].T, "bqkv": a["attn_b_qkv"][:2 * D].reshape(2 * KC, P).T,
        "bv": a["attn_b_qkv"][2 * D:].reshape(1, D), "woutT": a["attn_W_out"].T,
        "bout": a["attn_b_out"].reshape(1, D), "w1": a["ffn_W1"], "b1": a["ffn_b1"].reshape(FC, P).T,
        "ar1": np.concatenate([a["ffn_A1"].transpose(1, 0, 2).reshape(D, ER), a["ffn_R1"]], 1),
        "bl1": a["ffn_B1"].reshape(ER, FF), "w2": a["ffn_W2"], "b2": a["ffn_b2"].reshape(1, D),
        "ar2": np.concatenate([a["ffn_A2"].transpose(1, 0, 2).reshape(FF, ER), a["ffn_R2"]], 1),
        "bl2": a["ffn_B2"].reshape(ER, D),
    }
    nc = bacc.Bacc("TRN2", target_bir_lowering=False, num_devices=1)
    arrays, args = {}, []
    for name in _NAMES:
        arr = np.ascontiguousarray(laid[name])
        arrays[f"in_{name}"] = arr
        args.append(nc.dram_tensor(f"in_{name}", arr.shape, mybir.dt.from_np(arr.dtype), kind="ExternalInput").ap())
    args.append(nc.dram_tensor("out", (T, D), F32, kind="ExternalOutput").ap())
    build_program(nc, *args)
    r = run_bass_kernel_spmd(nc, [arrays], core_ids=[0])
    return r.results[0]["out"].reshape(B, S, D)
```

```python
from contextlib import ExitStack

import concourse.bass as bass
from concourse import mybir

P = 128
F32 = mybir.dt.float32
F32R = mybir.dt.float32r
BF16 = mybir.dt.bfloat16
ALU = mybir.AluOpType
ACT = mybir.ActivationFunctionType
AX = mybir.AxisListType.X

B, S, D = 2, 2048, 256
NH, HD = 16, 16
FF = 1024
E, R = 3, 8
ER = E * R
ZC = ER + E
ZP = ZC + 1
LR = 96
KC, FC = D // P, FF // P
T = B * S
BLK = 512
TT = BLK // P
NBLK = T // BLK
EPS = 1e-5
NEG = -3.0e38
GH = 4
NG = B * NH // GH
NPART = 3
QK_ROWS = 6 * HD
ST_ROWS = QK_ROWS + NPART
NJ = S // BLK
KT = [(J, t) for J in range(NJ) for t in range(4 * (J + 1))]
NKT = len(KT)
P_BUFS, PV_LAG = 4, 2
LAST_OF_J = {n: KT[n][0] for n in range(NKT) if n + 1 == NKT or KT[n + 1][0] != KT[n][0]}
FIRST_OF_J = {n: KT[n][0] for n in range(NKT) if KT[n][1] == 0}


def max_units():
    units = []
    for J in range(NJ):
        for r in range(4):
            i = 4 * J + r
            for h in range(GH):
                for c in range(J):
                    units.append((J, i, h, 1, c, BLK, False))
            together = {0: 4, 1: 2, 2: 1, 3: 1}[r]
            for h in range(0, GH, together):
                units.append((J, i, h, together, J, (r + 1) * P, True))
    return units


MU = max_units()
NMU = len(MU)
LAST_MU = {w: MU[w][0] for w in range(NMU) if w + 1 == NMU or MU[w + 1][0] != MU[w][0]}
S_BUFS = 3
T_LAG = 3


def max_events():
    events = []
    for w in range(NMU):
        events.append(("logits", w))
        if w - T_LAG in LAST_MU:
            events.append(("turn", LAST_MU[w - T_LAG]))
    return events + [("turn", NJ - 1)]


EV = max_events()
NEV = len(EV)
assert NEV % S_BUFS == 0
FIRST_SLOT = 7
SLOTS_OF_TILE = 3


def event_slots():
    slots, done = [], 0
    for u in range(SLOTS_OF_TILE * NKT):
        want = min(NEV, max(0, (u - FIRST_SLOT) * NEV // (SLOTS_OF_TILE * NKT - FIRST_SLOT - 2)))
        slots.append(range(done, want))
        done = want
    slots[-1] = range(slots[-1].start, NEV)
    return slots


SLOTS = event_slots()


def alone(eng):
    eng.nop(nofuse=True)


def start_at_one(eng, sems):
    for s in sems:
        eng.sem_inc(s, 1)


def until(eng, sem, count):
    if not (isinstance(count, int) and count <= 0):
        eng.wait_ge(sem, count + 1)


def batch_of(nc, pair):
    return nc.s_assert_within(pair >> 1, 0, B - 1,
                              skip_runtime_bounds_check_because="there are NBLK / 2 = 4 pairs, two of each batch")


def by_blocks(step):
    def run(eng):
        with eng.Fori(0, (NBLK - 2) // 2) as k:
            step(k * 2, 0, k, k, True)
            step(k * 2 + 1, 1, k, k + 1, True)
        step(NBLK - 2, 0, NBLK // 2 - 1, NBLK // 2 - 1, True)
        step(NBLK - 1, 1, NBLK // 2 - 1, None, False)
    return run


def build_program(nc, x, cT, wmod, wqkvT, bqkv, bv, woutT, bout, w1, b1, ar1, bl1, w2, b2, ar2, bl2, out):
    qk_parts = nc.dram_tensor("qk_parts", [2, NPART, D, T], BF16, kind="Internal").ap()
    o_rows = nc.dram_tensor("o_rows", [NH, HD, T], F32, kind="Internal").ap()
    rden_rows = nc.dram_tensor("rden_rows", [NH, T], F32, kind="Internal").ap()

    with ExitStack() as whole:
        def sb(ctx, name, shape, dt=F32):
            return ctx.enter_context(nc.sbuf_tensor(name, shape, dt))

        def sem(name):
            return whole.enter_context(nc.semaphore(name))

        ps = whole.enter_context(nc.psum_tensor("ps", [P, 8, BLK], F32))
        def pair_of(ctx, name, shape):
            return tuple(sb(ctx, f"{name}_{x}", shape, F32R) for x in ("hi", "lo"))

        w1_p = pair_of(whole, "w1", [P, KC, FF])
        w2_p = pair_of(whole, "w2", [P, FC, D + ZP])
        wout_p = pair_of(whole, "wout", [P, KC, D])
        ar1_p = pair_of(whole, "ar1", [P, KC, ZP])
        bl1_s = sb(whole, "bl1_s", [LR, FF], F32R)
        bl2_s = sb(whole, "bl2_s", [LR, D], F32R)
        b1_sb = sb(whole, "b1_sb", [P, FC])
        gates = sb(whole, "gates", [P, 2, B, D])
        bout_sb = sb(whole, "bout_sb", [P, D])
        b2_sb = sb(whole, "b2_sb", [P, D])
        boutg = sb(whole, "boutg", [P, B, D])
        b2g = sb(whole, "b2g", [P, B, D])
        mod = sb(whole, "mod", [P, B, 4, KC])
        ident = sb(whole, "ident", [P, P])
        ident_bf = sb(whole, "ident_bf", [P, P], BF16)
        mask_k = sb(whole, "mask_k", [P, P], BF16)
        mask_q = sb(whole, "mask_q", [P, P], BF16)

        den = sb(whole, "den", [P, 2, 64])
        rden = sb(whole, "rden", [P, 2, 64])

        v_scope = whole.enter_context(ExitStack())
        v_nat = sb(v_scope, "v_nat", [P, T // P, D])
        proj = ExitStack()
        wqkv_p = pair_of(proj, "wqkv", [P, KC, 3 * D])
        bq_sb = sb(proj, "bq_sb", [P, 2 * KC])
        bv_sb = sb(proj, "bv_sb", [P, D])
        xs1 = sb(proj, "xs1", [P, 2, TT, D])
        w1_full = sb(proj, "w1_full", [P, KC, FF])
        w2_full = sb(proj, "w2_full", [P, FC, D + ZP])
        xb_in = x.rearrange("(n t p) d -> n p t d", t=TT, p=P)

        w_loaded, padded_loaded, ffn_loaded, zeroed, highs = (
            sem(n) for n in ("w_loaded", "padded_loaded", "ffn_loaded", "zeroed", "highs"))
        w_in = [sem("c_in"), sem("wmod_in"), sem("wqkv_in")]
        cols_done, rows_done = sem("cols_done"), sem("rows_done")
        exp_c, dve0, pool0, act0 = sem("exp_c"), sem("dve0"), sem("pool0"), sem("act0")
        rden_stored = sem("rden_stored")
        x_in = [sem(f"x_in{q}") for q in range(2)]
        parts_stored = [sem(f"parts_stored{q}") for q in range(2)]
        ffn_high, ffn_low = sem("ffn_high"), sem("ffn_low")
        (var_done, std_done, xhat_done, xT_done, h_out, h_lo, qk_done, qk_out, v_done, v_out, rest1_done,
         part2_done, part3_done, dve1) = stage2 = [sem("s2_" + n) for n in (
             "var_done", "std_done", "xhat_done", "xT_done", "h_out", "h_lo", "qk_done", "qk_out",
             "v_done", "v_out", "rest1_done", "part2_done", "part3_done", "dve")]
        o_in = [sem(f"o_in{q}") for q in range(2)]
        x2_in = [sem(f"x2_in{q}") for q in range(2)]
        y_stored = [sem(f"y_stored{q}") for q in range(2)]
        (o_norm, o_hi, o_lo, p_done, xbias_done, x1_done, x1b_done, var2, std2, xhat2, xT2, h2_out, h2_lo,
         z1_done, z1_sub, z1_exp, zg1_done, zg1_turned, zg1_copied, f1_done, f1_out, hid_lo_done,
         z2_done, z2_sub, z2_exp, zg2_done, zg2_turned, zg2_copied, y_psum, y_gated, y_based,
         y_done, dve3) = stage4 = [
             sem("s4_" + n) for n in (
                 "o_norm", "o_hi", "o_lo", "p_done", "xbias_done", "x1_done", "x1b_done", "var", "std",
                 "xhat", "xT", "h_out", "h_lo", "z1_done", "z1_sub", "z1_exp", "zg1_done", "zg1_turned",
                 "zg1_copied", "f1_done", "f1_out", "hid_lo_done", "z2_done", "z2_sub", "z2_exp",
                 "zg2_done", "zg2_turned", "zg2_copied", "y_psum", "y_gated", "y_based",
                 "y_done", "dve")]
        credited = [rden_stored, ffn_high, *x_in, *parts_stored, *stage2, *o_in, *x2_in, *y_stored, *stage4]
        with ExitStack() as tmp, nc.Block() as block:
            c_sb = sb(tmp, "c_sb", [P, KC, B])
            ec = sb(tmp, "ec", [P, KC, B])
            silu = sb(tmp, "silu", [P, KC, B])
            silu_wide = sb(tmp, "silu_wide", [P, KC, B, P])
            ones = sb(tmp, "ones", [P, P])
            zeros = sb(tmp, "zeros", [P, P])
            wmod_sb = sb(tmp, "wmod_sb", [P, KC, 6 * D])
            wqkv_sb = sb(tmp, "wqkv_sb", [P, KC, 3 * D])
            wout_sb = sb(tmp, "wout_sb", [P, KC, D])
            ar1_sb = sb(tmp, "ar1_sb", [P, KC, ZP])
            bl1_sb = sb(tmp, "bl1_sb", [LR, FF])
            bl2_sb = sb(tmp, "bl2_sb", [LR, D])
            loads = [
                (c_sb[:], cT.rearrange("(k p) b -> p k b", p=P)),
                (wmod_sb[:], wmod.rearrange("(k p) n -> p k n", p=P)),
                (wqkv_sb[:], wqkvT.rearrange("(k p) n -> p k n", p=P)),
                (bq_sb[:], bqkv), (bv_sb[:], bv.broadcast_to((P, D))),
                (wout_sb[:], woutT.rearrange("(k p) n -> p k n", p=P)),
                (bout_sb[:], bout.broadcast_to((P, D))),
                (b1_sb[:], b1), (b2_sb[:], b2.broadcast_to((P, D))),
            ]
            ffn_loads = [
                (w1_full[:], w1.rearrange("(k p) n -> p k n", p=P)),
                (w2_full[:, :, 0:D], w2.rearrange("(k p) n -> p k n", p=P)),
                (w2_full[:, :, D:D + ZC], ar2.rearrange("(k p) n -> p k n", p=P)),
            ]
            padded_loads = [
                (ar1_sb[:, :, 0:ZC], ar1.rearrange("(k p) n -> p k n", p=P)),
            ] + [(t[r0:r0 + ER], src) for t, src in ((bl1_sb, bl1), (bl2_sb, bl2)) for r0 in (0, 32, 64)]
            splits = [(wqkv_sb, wqkv_p), (wout_sb, wout_p), (ar1_sb, ar1_p)]

            @block.sync
            def _(sp):
                for n, (dst, src) in enumerate(loads):
                    sp.dma_start(dst, src).then_inc(w_in[n] if n < 3 else w_loaded, 16)
                start_at_one(sp, credited)
                for n in range(2):
                    sp.dma_start(xs1[:, n], xb_in[n]).then_inc(x_in[n], 16)
                sp.wait_ge(zeroed, 4)
                for dst, src in padded_loads:
                    sp.dma_start(dst, src).then_inc(padded_loaded, 16)
                for dst, src in ffn_loads:
                    sp.dma_start(dst, src).then_inc(ffn_loaded, 16)

            @block.gpsimd
            def _(pool):
                pool.memset(ones[:], 1.0).then_inc(pool0, 1)
                pool.memset(zeros[:], 0.0).then_inc(pool0, 1)
                pool.wait_ge(pool0, 2)
                for dst in (ident, ident_bf):
                    pool.affine_select(out=dst[:], in_=ones[:], compare_op=ALU.is_equal, fill=0.0, base=0,
                                       pattern=[[-1, P]], channel_multiplier=1).then_inc(pool0, 1)
                pool.affine_select(out=mask_k[:], in_=zeros[:], compare_op=ALU.is_ge, fill=NEG, base=0,
                                   pattern=[[1, P]], channel_multiplier=-1).then_inc(pool0, 1)
                pool.affine_select(out=mask_q[:], in_=zeros[:], compare_op=ALU.is_ge, fill=NEG, base=0,
                                   pattern=[[-1, P]], channel_multiplier=1).then_inc(pool0, 1)

            @block.scalar
            def _(act):
                act.wait_ge(w_in[0], 16)
                act.activation(ec[:], c_sb[:], ACT.Exp, scale=-1.0).then_inc(exp_c, 1)
                for n, (full, (hi, _)) in enumerate(splits):
                    if n == 0:
                        act.wait_ge(w_in[2], 16)
                    if n == 1:
                        act.wait_ge(w_loaded, 16 * (len(loads) - 3))
                    if n == 2:
                        act.wait_ge(padded_loaded, 16 * len(padded_loads))
                    act.copy(hi[:], full[:]).then_inc(highs, 1)
                for full, stack in ((bl1_sb, bl1_s), (bl2_sb, bl2_s)):
                    act.copy(stack[:], full[:]).then_inc(highs, 1)

            @block.tensor
            def _(pe):
                pe.wait_ge(dve0, 3)
                pe.wait_ge(w_in[1], 16)
                for v, i in enumerate((1, 0, 4, 3)):
                    for m in range(KC):
                        for k in range(KC):
                            col = i * D + m * P
                            last = pe.matmul(ps[:, 0, (v * KC + m) * B:(v * KC + m + 1) * B],
                                             wmod_sb[:, k, col:col + P], silu[:, k, :],
                                             start=(k == 0), stop=(k == KC - 1))
                last.then_inc(cols_done, 1)
                pe.wait_ge(dve0, 3 + KC * B)
                for v, i in enumerate((2, 5)):
                    for b in range(B):
                        for k in range(KC):
                            last = pe.matmul(ps[:, 1 + v, b * D:(b + 1) * D], silu_wide[:, k, b, :],
                                             wmod_sb[:, k, i * D:(i + 1) * D],
                                             start=(k == 0), stop=(k == KC - 1))
                last.then_inc(rows_done, 1)

            @block.vector
            def _(dve):
                count = [0]

                def link(ins):
                    count[0] += 1
                    ins.then_inc(dve0, 1)
                    dve.wait_ge(dve0, count[0])

                for t in (w2_full[:, :, D + ZC:], ar1_sb[:], bl1_sb[:], bl2_sb[:]):
                    dve.memset(t, 0.0).then_inc(zeroed, 1)
                dve.wait_ge(exp_c, 1)
                dve.wait_ge(w_in[0], 16)
                link(dve.tensor_scalar(ec[:], ec[:], 1.0, None, ALU.add))
                link(dve.reciprocal(ec[:], ec[:]))
                link(dve.tensor_tensor(silu[:], c_sb[:], ec[:], ALU.mult))
                dve.wait_ge(pool0, 2)
                for k in range(KC):
                    for b in range(B):
                        link(dve.tensor_scalar(silu_wide[:, k, b, :], ones[:], silu[:, k, b:b + 1], None,
                                               ALU.mult))
                dve.wait_ge(w_loaded, 16 * (len(loads) - 3))
                link(dve.tensor_scalar(bq_sb[:, 0:KC], bq_sb[:, 0:KC], HD ** -0.5, None, ALU.mult))
                dve.wait_ge(cols_done, 1)
                cols = ps[:, 0, 0:4 * KC * B].rearrange("p (v m b) -> p v m b", v=4, m=KC)
                for v in range(4):
                    link(dve.tensor_scalar(mod[:, :, v, :].rearrange("p b m -> p m b"), cols[:, v],
                                           1.0 - v % 2, None, ALU.add))
                for n, (full, (hi, lo)) in enumerate(splits):
                    dve.wait_ge(highs, n + 1)
                    link(dve.tensor_tensor(lo[:], full[:], hi[:].bitcast(F32), ALU.subtract))
                for n, (full, stack) in enumerate(((bl1_sb, bl1_s), (bl2_sb, bl2_s))):
                    dve.wait_ge(highs, len(splits) + n + 1)
                    rows = slice(32, 32 + ER)
                    link(dve.tensor_tensor(stack[rows], full[rows], stack[rows].bitcast(F32), ALU.subtract))
                dve.wait_ge(rows_done, 1)
                for v in range(2):
                    link(dve.tensor_copy(gates[:, v].rearrange("p b d -> p (b d)"), ps[:, 1 + v, :]))

        PASSES = ((0, 0), (0, 1), (1, 0))

        def product(pe, out, lhs, rhs, chunks, start=True, stop=True):
            for k in range(chunks):
                for n, (a, b) in enumerate(PASSES):
                    last = pe.matmul(out, lhs(a, k), rhs(b, k), start=(start and k == 0 and n == 0),
                                     stop=(stop and k == chunks - 1 and n == len(PASSES) - 1))
            return last

        def statistics(dve, link, xs, stats, mv, var_done):
            for t in range(TT):
                link(dve.bn_stats(stats[:, t, :], xs[:, t, :]), wait=(t == TT - 1))
            alone(dve)
            for t in range(TT - 1):
                link(dve.bn_aggr(mv[:, t, :], stats[:, t, :]), wait=False)
            dve.bn_aggr(mv[:, TT - 1, :], stats[:, TT - 1, :]).then_inc(var_done, 1)

        def standardise(dve, link, f, xs, mv, rstd, xhat, std_done, xhat_done, turned):
            until(dve, std_done, f + 1)
            link(dve.reciprocal(rstd[:], rstd[:]))
            until(dve, *turned)
            for t in range(TT):
                last = dve.tensor_scalar(xhat[:, t, :], xs[:, t, :], mv[:, t, 0:1], rstd[:, t:t + 1],
                                         ALU.subtract, ALU.mult)
                if t < TT - 1:
                    link(last, wait=False)
            last.then_inc(xhat_done, 1)

        LN_LINKS = TT + TT - 1 + 1 + TT - 1

        with ExitStack() as tmp, nc.Block() as block:
            xs = xs1
            stats = sb(tmp, "stats", [P, TT, 6])
            mv = sb(tmp, "mv", [P, TT, 2])
            rstd = sb(tmp, "rstd", [P, TT])
            eps = sb(tmp, "eps", [P, 1])
            xhat = sb(tmp, "xhat", [P, TT, D])
            hf = sb(tmp, "hf", [P, KC, BLK])
            hT = pair_of(tmp, "hT", [P, 2, KC, BLK])
            qkf = sb(tmp, "qkf", [P, 2 * KC, BLK])
            rest = sb(tmp, "rest", [P, 2 * KC, BLK])
            parts = sb(tmp, "parts", [P, 2, NPART, 2 * KC, BLK], BF16)
            eps_set = sem("eps_set")
            T_BANK, V_BANK, QK_BANK = 0, 2, 4

            def has_far(n):
                return not (isinstance(n, int) and n >= NBLK - 2)

            @block.sync
            def _(sp):
                def load(n, q):
                    until(sp, xhat_done, n - 1)
                    alone(sp)
                    sp.dma_start(xs[:, q], xb_in[n]).then_inc(x_in[q], 16)

                def store(n, q):
                    for c in range(2 * KC):
                        if c % KC == 0:
                            until(sp, part3_done, n * 2 + 1 + c // KC)
                            alone(sp)
                        dst = qk_parts[c // KC, :, c % KC * P:(c % KC + 1) * P, bass.ds(n * BLK, BLK)]
                        sp.dma_start(dst.rearrange("a p t -> p a t"),
                                     parts[:, q, :, c, :]).then_inc(parts_stored[q], 16)

                load(2, 0)
                with sp.Fori(0, (NBLK - 4) // 2) as k:
                    load(k * 2 + 3, 1)
                    store(k * 2, 0)
                    load(k * 2 + 4, 0)
                    store(k * 2 + 1, 1)
                load(NBLK - 1, 1)
                for n in range(NBLK - 4, NBLK):
                    store(n, n % 2)
                for q in range(2):
                    until(sp, parts_stored[q], 16 * 2 * KC * NBLK // 2)

            @block.tensor
            def _(pe):
                def turn(f, p):
                    until(pe, xhat_done, f + 1)
                    until(pe, h_out, f * 2 * KC)
                    for k in range(KC):
                        for t in range(TT):
                            last = pe.transpose(ps[:, T_BANK + k, t * P:(t + 1) * P],
                                                xhat[:, t, k * P:(k + 1) * P], ident[:])
                        last.then_inc(xT_done, 1)

                def step(n, q, nb, fb, front):
                    if front:
                        turn(n + 1, 1 - q)
                    until(pe, h_lo, n + 1)
                    for c in range(2 * KC):
                        if c == 0:
                            until(pe, qk_out, n * 4 * KC)
                        product(pe, ps[:, QK_BANK + c, :], lambda a, k: wqkv_p[a][:, k, c * P:(c + 1) * P],
                                lambda a, k: hT[a][:, q, k, :], KC).then_inc(qk_done, 1)
                    until(pe, v_out, n)
                    for t in range(TT):
                        last = product(pe, ps[:, V_BANK + t // 2, t % 2 * D:(t % 2 + 1) * D],
                                       lambda a, k: hT[a][:, q, k, t * P:(t + 1) * P],
                                       lambda a, k: wqkv_p[a][:, k, 2 * D:], KC)
                    last.then_inc(v_done, 1)

                turn(0, 0)
                by_blocks(step)(pe)

            @block.scalar
            def _(act):
                def root(f):
                    until(act, var_done, f + 1)
                    act.activation(rstd[:], mv[:, :, 1], ACT.Sqrt, bias=eps[:]).then_inc(std_done, 1)

                def modulate(f, p, fb):
                    b = batch_of(nc, fb)
                    for k in range(KC):
                        until(act, xT_done, f * KC + k + 1)
                        until(act, v_done, f - 1)
                        until(act, h_lo, f)
                        alone(act)
                        for out in (hf[:, k, :], hT[0][:, p, k, :]):
                            act.activation(out, ps[:, T_BANK + k, :], ACT.Identity,
                                           bias=mod[:, bass.ds(b, 1), 1, k],
                                           scale=mod[:, bass.ds(b, 1), 0, k]).then_inc(h_out, 1)

                def step(n, q, nb, fb, front):
                    if front:
                        modulate(n + 1, 1 - q, fb)
                    until(act, rest1_done, n)
                    until(act, parts_stored[q], (n >> 1) * (16 * 2 * KC))
                    for c in range(2 * KC):
                        if c == KC and has_far(n):
                            root(n + 2)
                        until(act, qk_done, n * 2 * KC + c + 1)
                        for out in (qkf[:, c, :], parts[:, q, 0, c, :]):
                            act.activation(out, ps[:, QK_BANK + c, :], ACT.Identity,
                                           bias=bq_sb[:, c:c + 1],
                                           scale=(HD ** -0.5 if c < KC else 1.0)).then_inc(qk_out, 1)

                act.wait_ge(eps_set, 1)
                root(0)
                root(1)
                modulate(0, 0, 0)
                by_blocks(step)(act)

            @block.gpsimd
            def _(pool):
                def step(n, q, nb, fb, front):
                    pieces = [tuple(w[:].rearrange("p k f -> p (k f)")[:, bass.ds(n * width, width)]
                                    for w in (*pair, full))
                              for pair, full, width in ((w1_p, w1_full, KC * FF // NBLK),
                                                        (w2_p, w2_full, FC * (D + ZP) // NBLK))]
                    for hi, _, full in pieces:
                        pool.tensor_copy(hi, full).then_inc(ffn_high, 1)
                    until(pool, ffn_high, 2 * (n + 1))
                    alone(pool)
                    for hi, lo, full in pieces:
                        pool.tensor_tensor(lo, full, hi.bitcast(F32), ALU.subtract).then_inc(ffn_low, 1)
                    until(pool, part2_done, n + 1)
                    alone(pool)
                    for cs in (slice(0, KC), slice(KC, 2 * KC)):
                        pool.tensor_tensor(parts[:, q, 2, cs], rest[:, cs], parts[:, q, 1, cs],
                                           ALU.subtract).then_inc(part3_done, 1)

                pool.wait_ge(ffn_loaded, 16 * 3)
                by_blocks(step)(pool)
                pool.wait_ge(ffn_low, 2 * NBLK)

            @block.vector
            def _(dve):
                def linker(base):
                    count = [0]

                    def link(ins, wait=True):
                        count[0] += 1
                        ins.then_inc(dve1, 1)
                        if wait:
                            until(dve, dve1, base + count[0])
                    return link

                def normalise(f, p, xf):
                    until(dve, x_in[p], (xf + 1) * 16)
                    link = linker(f * LN_LINKS)
                    statistics(dve, link, xs[:, p], stats, mv, var_done)
                    standardise(dve, link, f, xs[:, p], mv, rstd, xhat, std_done, xhat_done, (xT_done, f * KC))

                def low(f, p):
                    until(dve, h_out, (f + 1) * 2 * KC)
                    dve.tensor_tensor(hT[1][:, p], hf[:], hT[0][:, p].bitcast(F32),
                                      ALU.subtract).then_inc(h_lo, 1)

                def step(n, q, nb, fb, front):
                    if has_far(n):
                        normalise(n + 2, q, nb + 1)
                    if front:
                        low(n + 1, 1 - q)
                    until(dve, qk_out, (n + 1) * 4 * KC)
                    until(dve, part3_done, n * 2)
                    dve.tensor_tensor(rest[:], qkf[:], parts[:, q, 0], ALU.subtract).then_inc(rest1_done, 1)
                    until(dve, rest1_done, n + 1)
                    dve.tensor_copy(parts[:, q, 1], rest[:]).then_inc(part2_done, 1)
                    until(dve, v_done, n + 1)
                    dve.tensor_tensor(v_nat[:, bass.ds(n * TT, TT), :],
                                      ps[:, V_BANK:V_BANK + 2, :].rearrange("p a (t d) -> p (a t) d", t=2),
                                      bv_sb[:].unsqueeze(1).broadcast_to((P, TT, D)), ALU.add).then_inc(v_out, 1)

                dve.memset(eps[:], EPS).then_inc(eps_set, 1)
                normalise(0, 0, 0)
                normalise(1, 1, 0)
                low(0, 0)
                by_blocks(step)(dve)
        proj.close()

        k_in, q_in, m_in = ([[sem(f"{n}_in{c}{J}") for J in range(NJ)] for c in range(2)] for n in "kqm")
        st_done, exp_done, pv_done, max_mm, max_red = (
            sem(n) for n in ("st_done", "exp_done", "pv_done", "max_mm", "max_red"))
        m_parts, gated = sem("m_parts"), sem("gated")
        o_out, v_wide, rden_done, ones_set = sem("o_out"), sem("v_wide"), sem("rden_done"), sem("ones_set")
        o_stored = [sem(f"o_stored{q}") for q in range(2)]
        den_in = [sem(f"den_in{q}") for q in range(2)]
        dve2 = sem("dve2")
        K_DMAS, Q_DMAS, O_DMAS = 6, 6, GH

        def invert(dve, s, c):
            for q in range(2):
                dve.wait_ge(den_in[q], (s + 1) * 32 * O_DMAS)
            until(dve, rden_stored, s * 16 * NJ)
            dve.reciprocal(rden[:, c, :], den[:, c, :]).then_inc(rden_done, 1)

        def store_rden(sp, s, c, hs):
            sp.wait_ge(rden_done, s + 1)
            for J in range(NJ):
                sp.dma_start(rden_rows[bass.ds(hs * GH, GH), c * S + J * BLK:c * S + (J + 1) * BLK],
                             rden[32 * J:32 * J + 32, c, :]).then_inc(rden_stored, 16)

        with ExitStack() as tmp, nc.Block() as block:
            kst = [sb(tmp, f"kst{q}", [P, NJ, GH, BLK], BF16) for q in range(2)]
            qst = [sb(tmp, f"qst{q}", [P, NJ, GH, BLK], BF16) for q in range(2)]
            vw = sb(tmp, "vw", [P, 2, S // P, GH, 2 * HD])
            prob = sb(tmp, "prob", [P, P_BUFS, GH, BLK])
            mx = sb(tmp, "mx", [P, GH, 4, NJ])
            negm = sb(tmp, "negm", [P, 2, GH * 4])
            mparts = sb(tmp, "mparts", [P, NPART, GH * 4], BF16)
            mT = sb(tmp, "mT", [NPART * GH * 4, NJ, P], BF16)
            o_sb = sb(tmp, "o_sb", [P, 2, BLK])
            S_BANK, O_BANK = 4, 7

            def load_q(sp, g, hg, J):
                c = g % 2
                for row, a in enumerate((0, 0, 0, 1, 1, 2)):
                    src = qk_parts[0, a, bass.ds(hg * (GH * HD), GH * HD),
                                   c * S + J * BLK:c * S + (J + 1) * BLK].rearrange("(h r) t -> r h t", r=HD)
                    sp.dma_start(qst[c][row * HD:(row + 1) * HD, J],
                                 src).then_inc(q_in[c][J], 16)

            def load_k(sp, g, hg, J):
                c = g % 2
                for row, a in enumerate((0, 1, 2, 0, 1, 0)):
                    src = qk_parts[1, a, bass.ds(hg * (GH * HD), GH * HD),
                                   c * S + J * BLK:c * S + (J + 1) * BLK].rearrange("(h r) t -> r h t", r=HD)
                    sp.dma_start(kst[c][row * HD:(row + 1) * HD, J],
                                 src).then_inc(k_in[c][J], 16)

            def bound_gates(dve):
                count = [0]

                def link(ins):
                    count[0] += 1
                    ins.then_inc(gated, 1)
                    dve.wait_ge(gated, count[0])

                sign, size = (t[:].rearrange("p b d -> p (b d)") for t in (boutg, b2g))
                for v in range(2):
                    gate = gates[:, v].rearrange("p b d -> p (b d)")
                    link(dve.tensor_scalar(sign, gate, 0.0, 2.0, ALU.is_ge, ALU.mult))
                    link(dve.scalar_tensor_tensor(out=size, in0=gate, scalar=-1.0, in1=gate,
                                                  op0=ALU.mult, op1=ALU.max))
                    link(dve.tensor_scalar(size, size, 0.25, None, ALU.max))
                    link(dve.scalar_tensor_tensor(out=gate, in0=sign, scalar=-1.0, in1=size,
                                                  op0=ALU.add, op1=ALU.mult))
                for v, (bias, out) in enumerate(((bout_sb, boutg), (b2_sb, b2g))):
                    for b in range(B):
                        link(dve.tensor_tensor(out[:, b], bias[:], gates[:, v, b], ALU.mult))

            def sync_step(sp, s, c, hs, cur, nxt, far):
                nhs = hs + c
                nc_ = 1 - c
                for J in range(NJ):
                    if nxt:
                        sp.wait_ge(max_red, (s + 1) * NEV + EV.index(("turn", J)) + 1)
                        for a in range(NPART):
                            sp.dma_start(qst[nc_][QK_ROWS + a:QK_ROWS + a + 1, J],
                                         mT[a * 16:(a + 1) * 16, J, :]).then_inc(m_in[nc_][J], 16)
                    if cur and far and J < NJ - 1:
                        sp.wait_ge(st_done, s * 2 * NKT + 2 * (1 + max(n for n in range(NKT) if KT[n][0] == J)))
                        load_q(sp, c, hs + 1, J)
                    if cur and far and J == NJ - 1:
                        sp.wait_ge(st_done, (s + 1) * 2 * NKT)
                        for j in range(NJ):
                            load_k(sp, c, hs + 1, j)
                        load_q(sp, c, hs + 1, J)
                    if cur:
                        sp.wait_ge(o_out, s * NJ + J + 1)
                        cols = slice(c * S + J * BLK, c * S + (J + 1) * BLK)
                        for h in range(GH):
                            sp.dma_start(o_rows[bass.ds(hs * GH + h, 1), :, cols]
                                         .rearrange("o r t -> (o r) t"),
                                         o_sb[2 * HD * h:2 * HD * h + HD, J % 2, :]
                                         ).then_inc(o_stored[J % 2], 16)
                            sp.dma_start(den[32 * J + 8 * h:32 * J + 8 * h + 8, c, :],
                                         o_sb[2 * HD * h + HD:2 * HD * h + HD + 1, J % 2, :]
                                         ).then_inc(den_in[J % 2], 16)
                    if cur and J == 1 and not (isinstance(s, int) and s == 0):
                        store_rden(sp, s - 1, 1 - c, hs - 1 + c)

            def tensor_step(pe, s, c, hs, cur, nxt):
                g, q, k = s + 1, qst[1 - c], kst[1 - c]

                def event(e):
                    kind, w = EV[e]
                    bank = S_BANK + e % S_BUFS
                    if not (isinstance(g, int) and g == 0 and e < S_BUFS):
                        pe.wait_ge(max_red, g * NEV + e - S_BUFS + 1)
                    if kind == "turn":
                        pe.wait_ge(m_parts, g * NJ + w + 1)
                        alone(pe)
                        pe.transpose(ps[0:NPART * 16, bank, 0:P // 2].bitcast(BF16),
                                     mparts[:].rearrange("p a x -> p (a x)"), ident_bf[:]).then_inc(max_mm, 1)
                        return
                    J, i, h0, nh, cb, width, diagonal = MU[w]
                    if w == 0 or MU[w - 1][0] != J:
                        pe.wait_ge(q_in[1 - c][J], loads(hs + c, Q_DMAS))
                        pe.wait_ge(k_in[1 - c][J], loads(hs + c, K_DMAS))
                    for h in range(nh):
                        at = ps[:, bank, h * width:(h + 1) * width]
                        last = pe.matmul(at, q[0:QK_ROWS, J, h0 + h, i % 4 * P:(i % 4 + 1) * P],
                                         k[0:QK_ROWS, cb, h0 + h, 0:width], start=True, stop=not diagonal)
                        if diagonal:
                            last = pe.matmul(at[:, width - P:width], ident_bf[:], mask_q[:],
                                             start=False, stop=True)
                    last.then_inc(max_mm, 1)

                def maxima(slot):
                    for e in SLOTS[slot]:
                        event(e)

                def logits(n, pair):
                    J, t = KT[n]
                    u = 2 * n + pair
                    skip = max(0, t - 4 * J) * P
                    width = BLK - skip
                    if isinstance(s, int) and s == 0 and u == 0:
                        pe.wait_ge(ones_set, 2)
                    if n in FIRST_OF_J and pair == 0:
                        pe.wait_ge(m_in[c][J], loads(hs, NPART))
                    if not (isinstance(s, int) and s == 0 and u < 2):
                        pe.wait_ge(exp_done, s * 2 * NKT + u - 1)
                    for h in range(2 * pair, 2 * pair + 2):
                        last = pe.matmul(ps[:, h, 0:width], kst[c][0:ST_ROWS, t // 4, h, t % 4 * P:(t % 4 + 1) * P],
                                         qst[c][0:ST_ROWS, J, h, skip:BLK],
                                         start=True, stop=(t < 4 * J))
                        if t >= 4 * J:
                            last = pe.matmul(ps[:, h, 0:P], ident_bf[:], mask_k[:], start=False, stop=True)
                    last.then_inc(st_done, 1)

                def values(n, s, c):
                    J, t = KT[n]
                    skip = max(0, t - 4 * J) * P
                    pe.wait_ge(exp_done, s * 2 * NKT + 2 * n + 2)
                    if n == 0:
                        pe.wait_ge(v_wide, s + 1)
                    if n in FIRST_OF_J and not (isinstance(s, int) and s == 0 and J == 0):
                        pe.wait_ge(o_out, s * NJ + J)
                    for h in range(GH):
                        last = pe.matmul(ps[32 * h:32 * h + 32, O_BANK, skip:BLK], vw[:, c, t, h, :],
                                         prob[:, n % P_BUFS, h, 0:BLK - skip],
                                         start=(t == 0), stop=(n in LAST_OF_J), tile_position=(0, 32 * h))
                    last.then_inc(pv_done, 1)

                if not cur:
                    for e in range(NEV):
                        event(e)
                    return
                for n in range(NKT):
                    logits(n, 0)
                    if nxt:
                        maxima(SLOTS_OF_TILE * n)
                    if n >= PV_LAG:
                        values(n - PV_LAG, s, c)
                    elif not (isinstance(s, int) and s == 0):
                        values(NKT + n - PV_LAG, s - 1, 1 - c)
                    if nxt:
                        maxima(SLOTS_OF_TILE * n + 1)
                    logits(n, 1)
                    if nxt:
                        maxima(SLOTS_OF_TILE * n + 2)
                if not nxt:
                    for n in range(NKT - PV_LAG, NKT):
                        values(n, s, c)

            def scalar_step(act, s, c, last_step):
                def copy_out(J, s):
                    act.wait_ge(pv_done, s * NKT + 1 + max(n for n in range(NKT) if KT[n][0] == J))
                    if J >= 2:
                        act.wait_ge(o_stored[J % 2], s * 32 * O_DMAS + 16 * O_DMAS)
                        act.wait_ge(den_in[J % 2], s * 32 * O_DMAS + 16 * O_DMAS)
                    elif not (isinstance(s, int) and s == 0):
                        act.wait_ge(o_stored[J % 2], s * 32 * O_DMAS)
                        act.wait_ge(den_in[J % 2], s * 32 * O_DMAS)
                    act.copy(o_sb[:, J % 2, :], ps[:, O_BANK, :]).then_inc(o_out, 1)

                for n in range(NKT):
                    J, t = KT[n]
                    width = BLK - max(0, t - 4 * J) * P
                    if not (isinstance(s, int) and s == 0 and n < P_BUFS):
                        act.wait_ge(pv_done, s * NKT + n - P_BUFS + 1)
                    for pair in range(2):
                        act.wait_ge(st_done, s * 2 * NKT + 2 * n + pair + 1)
                        act.activation(prob[:, n % P_BUFS, 2 * pair:2 * pair + 2, 0:width],
                                       ps[:, 2 * pair:2 * pair + 2, 0:width], ACT.Exp).then_inc(exp_done, 1)
                        if pair == 0 and n - PV_LAG in LAST_OF_J:
                            copy_out(LAST_OF_J[n - PV_LAG], s)
                        if pair == 0 and n == PV_LAG - 1 and not (isinstance(s, int) and s == 0):
                            copy_out(NJ - 1, s - 1)
                if last_step:
                    copy_out(NJ - 1, s)

            def vector_step(dve, s, c, hs, cur, nxt):
                g = s + 1
                count = [0]
                per_s = 4 * NJ

                def link(ins):
                    count[0] += 1
                    ins.then_inc(dve2, 1)
                    dve.wait_ge(dve2, g * per_s + count[0])

                def make_parts(J):
                    m = negm[:, 0, :]
                    link(dve.tensor_reduce(m.rearrange("p (h i) -> p h i", i=4), mx[:, :, :, 0:J + 1],
                                           AX, ALU.max, negate=True))
                    link(dve.tensor_copy(mparts[:, 0, :], m))
                    link(dve.tensor_tensor(negm[:, 1, :], m, mparts[:, 0, :], ALU.subtract))
                    link(dve.tensor_copy(mparts[:, 1, :], negm[:, 1, :]))
                    dve.tensor_tensor(mparts[:, 2, :], negm[:, 1, :], mparts[:, 1, :],
                                      ALU.subtract).then_inc(m_parts, 1)

                def copy_parts(J, bank):
                    if not (isinstance(g, int) and g == 0):
                        dve.wait_ge(m_in[c][J], loads(hs, NPART))
                    dve.tensor_copy(mT[:, J, :], ps[0:NPART * 16, bank, 0:P // 2].bitcast(BF16)
                                    ).then_inc(max_red, 1)

                if nxt:
                    for e in range(NEV):
                        kind, w = EV[e]
                        bank = S_BANK + e % S_BUFS
                        dve.wait_ge(max_mm, g * NEV + e + 1)
                        if kind == "turn":
                            copy_parts(w, bank)
                            continue
                        J, i, h0, nh, cb, width, _ = MU[w]
                        dve.tensor_reduce(mx[:, h0:h0 + nh, i % 4, cb],
                                          ps[:, bank, 0:nh * width].rearrange("p (h x) -> p h x", h=nh),
                                          AX, ALU.max).then_inc(max_red, 1)
                        if w in LAST_MU:
                            dve.wait_ge(max_red, g * NEV + e + 1)
                            make_parts(LAST_MU[w])
                        if w == NMU // 2 and not (isinstance(s, int) and s <= 0):
                            invert(dve, s - 1, 1 - c)
                    assert count[0] == per_s

            def loads(hs, dmas):
                return (hs + 1) * 16 * dmas

            def over_steps(eng, step):
                step(0, 0, 0, True)
                with eng.Fori(0, (NG - 2) // 2) as k:
                    step(k * 2 + 1, 1, k, True)
                    step(k * 2 + 2, 0, k + 1, True)
                step(NG - 1, 1, NG // 2 - 1, False)

            @block.sync
            def _(sp):
                for J in range(NJ):
                    load_q(sp, 0, 0, J)
                    load_k(sp, 0, 0, J)
                for J in range(NJ):
                    load_q(sp, 1, 0, J)
                    load_k(sp, 1, 0, J)
                sync_step(sp, -1, 1, -1, False, True, False)
                sync_step(sp, 0, 0, 0, True, True, True)
                with sp.Fori(0, (NG - 4) // 2) as k:
                    sync_step(sp, k * 2 + 1, 1, k, True, True, True)
                    sync_step(sp, k * 2 + 2, 0, k + 1, True, True, True)
                sync_step(sp, NG - 3, 1, NG // 2 - 2, True, True, True)
                sync_step(sp, NG - 2, 0, NG // 2 - 1, True, True, False)
                sync_step(sp, NG - 1, 1, NG // 2 - 1, True, False, False)
                until(sp, rden_stored, 16 * NJ * (NG - 1))
                for q in range(2):
                    sp.wait_ge(o_stored[q], 16 * O_DMAS * NJ // 2 * NG)
                    sp.wait_ge(den_in[q], 16 * O_DMAS * NJ // 2 * NG)

            @block.tensor
            def _(pe):
                tensor_step(pe, -1, 1, -1, False, True)
                over_steps(pe, lambda s, c, hs, nxt: tensor_step(pe, s, c, hs, True, nxt))

            @block.scalar
            def _(act):
                over_steps(act, lambda s, c, hs, nxt: scalar_step(act, s, c, not nxt))

            @block.vector
            def _(dve):
                vector_step(dve, -1, 1, -1, False, True)
                over_steps(dve, lambda s, c, hs, nxt: vector_step(dve, s, c, hs, True, nxt))
                bound_gates(dve)
                invert(dve, NG - 2, 0)

            @block.gpsimd
            def _(pool):
                for q in range(2):
                    pool.memset(kst[q][QK_ROWS:ST_ROWS], 1.0).then_inc(ones_set, 1)
                pool.wait_ge(ones_set, 2)
                pool.memset(vw[:, :, :, :, HD:].rearrange("p c t h d -> p (c t h) d"), 1.0).then_inc(pool0, 1)
                pool.wait_ge(pool0, 7)

                def widen(s, c, hs):
                    if not (isinstance(s, int) and s < 2):
                        pool.wait_ge(pv_done, (s - 1) * NKT)
                    nt = S // P
                    pool.tensor_copy(vw[:, c, :, :, 0:HD],
                                     v_nat[:, c * nt:(c + 1) * nt, bass.ds(hs * (GH * HD), GH * HD)]
                                     .rearrange("p t (h d) -> p t h d", d=HD)).then_inc(v_wide, 1)

                widen(0, 0, 0)
                widen(1, 1, 0)
                with pool.Fori(0, (NG - 2) // 2) as k:
                    widen(k * 2 + 2, 0, k + 1)
                    widen(k * 2 + 3, 1, k + 1)

        v_scope.close()

        out_b = out.rearrange("(n t p) d -> n p t d", t=TT, p=P)
        o_feat = o_rows.rearrange("h r t -> (h r) t")
        with ExitStack() as tmp, nc.Block() as block:
            xs = sb(tmp, "xs2", [P, 2, TT, D])
            o_raw = sb(tmp, "o_raw", [P, 2, KC, BLK])
            rd = sb(tmp, "rd", [P, 2, KC, BLK])
            oT = pair_of(tmp, "oT", [P, KC, BLK])
            x1 = sb(tmp, "x1", [P, 2, TT, D])
            x1b = sb(tmp, "x1b", [P, 2, TT, D])
            y = sb(tmp, "y", [P, 2, TT, D])
            y_low = sb(tmp, "y_low", [P, TT, D])
            stats = sb(tmp, "stats2", [P, TT, 6])
            mv = sb(tmp, "mv2", [P, TT, 2])
            rstd = sb(tmp, "rstd2", [P, TT])
            eps = sb(tmp, "eps2", [P, 1])
            xhat = sb(tmp, "xhat2", [P, TT, D])
            hf = sb(tmp, "hf2", [P, KC, BLK])
            hT = pair_of(tmp, "hT2", [P, 2, KC, BLK])
            HRING = 4
            hidf = sb(tmp, "hidf", [P, HRING, BLK])
            hid = pair_of(tmp, "hid", [P, FC, BLK])
            gmax = sb(tmp, "gmax", [P, TT])
            gexp = sb(tmp, "gexp", [P, TT, E])
            gsum = sb(tmp, "gsum", [P, TT])
            zf = sb(tmp, "zf", [P, TT, ER])
            zg = sb(tmp, "zg", [P, 2, TT, LR])
            zgT1 = sb(tmp, "zgT1", [LR, 2, BLK], F32R)
            zgT2 = sb(tmp, "zgT2", [LR, BLK], F32R)
            ready4 = sem("ready4")
            Y_BANK, T_BANK, H_BANK = 0, 4, 6

            def by_steps(step):
                def run(eng):
                    step(0, 0, 0, 0, False, True)
                    with eng.Fori(0, (NBLK - 2) // 2) as k:
                        step(k * 2 + 1, 1, k, k + 1, True, True)
                        step(k * 2 + 2, 0, k + 1, k + 1, True, True)
                    step(NBLK - 1, 1, NBLK // 2 - 1, None, True, False)
                return run

            @block.sync
            def _(sp):
                def load(n, q):
                    until(sp, o_lo, n - 1)
                    for k in range(KC):
                        sp.dma_start(o_raw[:, q, k, :],
                                     o_feat[k * P:(k + 1) * P, bass.ds(n * BLK, BLK)]).then_inc(o_in[q], 16)
                        sp.dma_start(rd[:, q, k, :],
                                     rden_rows[k * 8:(k + 1) * 8, bass.ds(n * BLK, BLK)].unsqueeze(1)
                                     .broadcast_to((8, HD, BLK))).then_inc(o_in[q], 16)
                    until(sp, x1_done, n - 1)
                    sp.dma_start(xs[:, q], xb_in[n]).then_inc(x2_in[q], 16)

                def store(n, q):
                    until(sp, y_done, n + 1)
                    sp.dma_start(out_b[n], y[:, q]).then_inc(y_stored[q], 16)

                load(0, 0)
                load(1, 1)
                store_rden(sp, NG - 1, 1, NG // 2 - 1)
                load(2, 0)
                until(sp, rden_stored, 16 * NJ * NG)
                with sp.Fori(0, (NBLK - 4) // 2) as k:
                    store(k * 2, 0)
                    load(k * 2 + 3, 1)
                    store(k * 2 + 1, 1)
                    load(k * 2 + 4, 0)
                store(NBLK - 4, 0)
                load(NBLK - 1, 1)
                for n in range(NBLK - 3, NBLK):
                    store(n, n % 2)
                for q in range(2):
                    until(sp, y_stored[q], 16 * NBLK // 2)

            @block.gpsimd
            def _(pool):
                def normalise_o(f, p, fb):
                    until(pool, o_in[p], (fb + 1) * 16 * 2 * KC)
                    alone(pool)
                    pool.tensor_tensor(o_raw[:, p], o_raw[:, p], rd[:, p], ALU.mult).then_inc(o_norm, 1)

                def biases(f, p, fb):
                    b = batch_of(nc, fb)
                    until(pool, x2_in[p], (fb + 1) * 16)
                    alone(pool)
                    pool.tensor_tensor(xs[:, p], xs[:, p], boutg[:, bass.ds(b, 1), :].broadcast_to((P, TT, D)),
                                       ALU.add).then_inc(xbias_done, 1)
                    until(pool, x1_done, f + 1)
                    until(pool, y_done, f - 1)
                    alone(pool)
                    pool.tensor_tensor(x1b[:, p], x1[:, p], b2g[:, bass.ds(b, 1), :].broadcast_to((P, TT, D)),
                                       ALU.add).then_inc(x1b_done, 1)

                def base_y(n, q):
                    until(pool, y_gated, n + 1)
                    until(pool, x1b_done, n + 1)
                    alone(pool)
                    pool.tensor_tensor(y[:, q], y[:, q], x1b[:, q], ALU.add).then_inc(y_based, 1)

                def step(n, q, nb, fb, back, front):
                    if front:
                        normalise_o(n + 1, 1 - q, fb)
                    if back:
                        base_y(n - 1, 1 - q)
                    if front:
                        biases(n + 1, 1 - q, fb)

                normalise_o(0, 0, 0)
                biases(0, 0, 0)
                by_steps(step)(pool)
                base_y(NBLK - 1, 1)

            @block.tensor
            def _(pe):
                def project_out(f):
                    until(pe, o_hi, f + 1)
                    until(pe, o_lo, f + 1)
                    until(pe, zg1_copied, f)
                    until(pe, zg2_copied, f - 1)
                    for t in range(TT):
                        last = product(pe, ps[:, T_BANK + t // 2, t % 2 * D:(t % 2 + 1) * D],
                                       lambda a, k: oT[a][:, k, t * P:(t + 1) * P],
                                       lambda a, k: wout_p[a][:, k, :], KC)
                    last.then_inc(p_done, 1)

                def turn(f):
                    until(pe, xhat2, f + 1)
                    for k in range(KC):
                        for t in range(TT):
                            last = pe.transpose(ps[:, T_BANK + k, t * P:(t + 1) * P],
                                                xhat[:, t, k * P:(k + 1) * P], ident[:])
                        last.then_inc(xT2, 1)

                def route_in(f, p):
                    until(pe, h2_out, (f + 1) * 2 * KC)
                    until(pe, h2_lo, f + 1)
                    for t in range(TT):
                        last = product(pe, ps[:, T_BANK, t * 32:t * 32 + ZP],
                                       lambda a, k: hT[a][:, p, k, t * P:(t + 1) * P],
                                       lambda a, k: ar1_p[a][:, k, :], KC)
                    last.then_inc(z1_done, 1)

                def turn_gated(v, n, ready, turned):
                    until(pe, ready, n + 1)
                    for t in range(TT):
                        last = pe.transpose(ps[0:LR, T_BANK + 1 - v, t * P:(t + 1) * P], zg[:, v, t, :],
                                            ident[:])
                    last.then_inc(turned, 1)

                def hidden(n, q, m):
                    until(pe, f1_out, n * 2 * FC + 2 * (m - 1) if m >= 2 else n * 2 * FC)
                    product(pe, ps[:, H_BANK + m % 2, :], lambda a, k: w1_p[a][:, k, m * P:(m + 1) * P],
                            lambda a, k: hT[a][:, q, k, :], KC, stop=False)

                def hidden_low_rank(q, m):
                    pe.matmul(ps[:, H_BANK + m % 2, :], bl1_s[:, m * P:(m + 1) * P], zgT1[:, q, :],
                              start=False, stop=True).then_inc(f1_done, 1)

                def down(n, t):
                    order = [(0, b, m) for m in range(FC) for b in range(2)] + [(1, 0, m) for m in range(FC)]
                    for e, (a, b, m) in enumerate(order):
                        if t == 0 and (a, b) != (0, 1):
                            if a == 0:
                                until(pe, f1_out, n * 2 * FC + 2 * (m + 1))
                            else:
                                until(pe, hid_lo_done, n * FC + m + 1)
                        last = pe.matmul(ps[:, Y_BANK + t, 0:D + ZP], hid[a][:, m, t * P:(t + 1) * P],
                                         w2_p[b][:, m, :], start=(e == 0), stop=(e == len(order) - 1))
                    return last

                def down_low_rank(n):
                    until(pe, zg2_copied, n + 1)
                    until(pe, y_gated, n + 1)
                    for t in range(TT):
                        last = pe.matmul(ps[:, Y_BANK + t, 0:D], zgT2[:, t * P:(t + 1) * P], bl2_s[:],
                                         start=True, stop=True)
                    last.then_inc(y_psum, 1)

                def step(n, q, nb, fb, back, front):
                    hidden(n, q, 0)
                    turn_gated(0, n, zg1_done, zg1_turned)
                    hidden(n, q, 1)
                    until(pe, zg1_copied, n + 1)
                    hidden_low_rank(q, 0)
                    hidden_low_rank(q, 1)
                    for m in range(2, FC):
                        hidden(n, q, m)
                        hidden_low_rank(q, m)
                        if m == 2 and back:
                            turn_gated(1, n - 1, zg2_done, zg2_turned)
                        if m == 3 and back:
                            down_low_rank(n - 1)
                        if m == 3 and front:
                            project_out(n + 1)
                    until(pe, y_done, n)
                    down(n, 0)
                    if front:
                        turn(n + 1)
                    down(n, 1)
                    down(n, 2)
                    if front:
                        route_in(n + 1, 1 - q)
                    down(n, 3).then_inc(z2_done, 1)

                project_out(0)
                turn(0)
                route_in(0, 0)
                by_steps(step)(pe)
                turn_gated(1, NBLK - 1, zg2_done, zg2_turned)
                down_low_rank(NBLK - 1)

            @block.scalar
            def _(act):
                def o_high(f, p):
                    until(act, o_norm, f + 1)
                    until(act, p_done, f)
                    act.copy(oT[0][:], o_raw[:, p]).then_inc(o_hi, 1)

                def root(f):
                    until(act, var2, f + 1)
                    act.activation(rstd[:], mv[:, :, 1], ACT.Sqrt, bias=eps[:]).then_inc(std2, 1)

                def modulate(f, p, fb):
                    b = batch_of(nc, fb)
                    for k in range(KC):
                        until(act, xT2, f * KC + k + 1)
                        until(act, h2_lo, f)
                        alone(act)
                        for out in (hf[:, k, :], hT[0][:, p, k, :]):
                            act.activation(out, ps[:, T_BANK + k, :], ACT.Identity,
                                           bias=mod[:, bass.ds(b, 1), 3, k],
                                           scale=mod[:, bass.ds(b, 1), 2, k]).then_inc(h2_out, 1)

                def exponentials(n, sub, exp_done):
                    until(act, sub, n + 1)
                    act.activation(gexp[:], gexp[:], ACT.Exp).then_inc(exp_done, 1)

                def gated_in(n, q):
                    until(act, zg1_turned, n + 1)
                    alone(act)
                    act.copy(zgT1[:, q, :], ps[0:LR, T_BANK + 1, :]).then_inc(zg1_copied, 1)

                def gated_down(n):
                    until(act, zg2_turned, n + 1)
                    until(act, y_psum, n)
                    alone(act)
                    act.copy(zgT2[:], ps[0:LR, T_BANK, :]).then_inc(zg2_copied, 1)

                def hidden(n, m):
                    until(act, f1_done, n * FC + m + 1)
                    if m == 0:
                        until(act, z2_done, n)
                    if m >= HRING:
                        until(act, hid_lo_done, n * FC + m - HRING + 1)
                    elif not (isinstance(n, int) and n == 0):
                        until(act, hid_lo_done, n * FC)
                    for out in (hidf[:, m % HRING, :], hid[0][:, m, :]):
                        act.activation(out, ps[:, H_BANK + m % 2, :], ACT.Relu,
                                       bias=b1_sb[:, m:m + 1]).then_inc(f1_out, 1)

                def step(n, q, nb, fb, back, front):
                    if back:
                        exponentials(n - 1, z2_sub, z2_exp)
                    if front:
                        o_high(n + 1, 1 - q)
                    gated_in(n, q)
                    for m in range(FC):
                        hidden(n, m)
                        if m == 2 and back:
                            gated_down(n - 1)
                        if m == 5 and front:
                            root(n + 1)
                    if front:
                        modulate(n + 1, 1 - q, fb)
                        exponentials(n + 1, z1_sub, z1_exp)

                act.wait_ge(ready4, 2)
                o_high(0, 0)
                root(0)
                modulate(0, 0, 0)
                exponentials(0, z1_sub, z1_exp)
                by_steps(step)(act)
                exponentials(NBLK - 1, z2_sub, z2_exp)
                gated_down(NBLK - 1)

            @block.vector
            def _(dve):
                X1_LINKS, ROUTE_LINKS, Y_LINKS = 1, 7, 1
                FRONT, REST = X1_LINKS + LN_LINKS + ROUTE_LINKS, ROUTE_LINKS + Y_LINKS
                made, base = [0], [0]

                def link(ins, wait=True):
                    made[0] += 1
                    ins.then_inc(dve3, 1)
                    if wait:
                        until(dve, dve3, base[0] + made[0])

                def low_o(f, p):
                    until(dve, o_hi, f + 1)
                    dve.tensor_tensor(oT[1][:], o_raw[:, p], oT[0][:].bitcast(F32), ALU.subtract).then_inc(o_lo, 1)

                def residual(f, p, fb):
                    b = batch_of(nc, fb)
                    until(dve, p_done, f + 1)
                    until(dve, x1b_done, f - 1)
                    link(dve.tensor_tensor(x1[:, p],
                                           ps[:, T_BANK:T_BANK + 2, :].rearrange("p a (t d) -> p (a t) d", t=2),
                                           gates[:, 0, bass.ds(b, 1), :].broadcast_to((P, TT, D)), ALU.mult))
                    until(dve, xbias_done, f + 1)
                    dve.tensor_tensor(x1[:, p], x1[:, p], xs[:, p], ALU.add).then_inc(x1_done, 1)
                    until(dve, x1_done, f + 1)
                    statistics(dve, link, x1[:, p], stats, mv, var2)

                def standardise_x1(f, p):
                    standardise(dve, link, f, x1[:, p], mv, rstd, xhat, std2, xhat2, (xT2, f * KC))

                def low(f, p):
                    until(dve, h2_out, (f + 1) * 2 * KC)
                    dve.tensor_tensor(hT[1][:, p], hf[:], hT[0][:, p].bitcast(F32),
                                      ALU.subtract).then_inc(h2_lo, 1)

                def route(v, z, n, done, sub, exp_done, zg_done):
                    lv = z[:, :, ER:ZC]
                    until(dve, done, n + 1)
                    link(dve.tensor_reduce(gmax[:], lv, AX, ALU.max))
                    dve.tensor_tensor(gexp[:], lv, gmax[:].unsqueeze(2).broadcast_to((P, TT, E)),
                                      ALU.subtract).then_inc(sub, 1)
                    until(dve, exp_done, n + 1)
                    link(dve.tensor_reduce(gsum[:], gexp[:], AX, ALU.add))
                    link(dve.reciprocal(gsum[:], gsum[:]))
                    link(dve.scalar_tensor_tensor(out=gexp[:], in0=gexp[:], scalar=1.0 / R,
                                                  in1=gsum[:].unsqueeze(2).broadcast_to((P, TT, E)),
                                                  op0=ALU.mult, op1=ALU.mult))
                    link(dve.tensor_tensor(zf[:].rearrange("p t (e r) -> p t e r", r=R),
                                           z[:, :, 0:ER].rearrange("p t (e r) -> p t e r", r=R),
                                           gexp[:].unsqueeze(3).broadcast_to((P, TT, E, R)), ALU.mult))
                    highs = [zg[:, v, :, r0:r0 + ER].bitcast(F32R) for r0 in (0, 32)]
                    for high in highs:
                        link(dve.tensor_copy(high, zf[:]), wait=(high is highs[1]))
                    dve.tensor_tensor(zg[:, v, :, 64:64 + ER].bitcast(F32R), zf[:], zg[:, v, :, 0:ER],
                                      ALU.subtract).then_inc(zg_done, 1)

                def route_in(n):
                    until(dve, zg1_turned, n)
                    route(0, ps[:, T_BANK, 0:TT * 32].rearrange("p (t c) -> p t c", c=32), n,
                          z1_done, z1_sub, z1_exp, zg1_done)

                def route_hidden(n):
                    until(dve, zg2_turned, n)
                    route(1, ps[:, Y_BANK:Y_BANK + TT, D:D + ZP], n, z2_done, z2_sub, z2_exp, zg2_done)

                def hid_low(n, m):
                    until(dve, f1_out, n * 2 * FC + 2 * m + 2)
                    if m == 0:
                        until(dve, z2_done, n)
                    dve.tensor_tensor(hid[1][:, m, :], hidf[:, m % HRING, :], hid[0][:, m, :].bitcast(F32),
                                      ALU.subtract).then_inc(hid_lo_done, 1)

                def gate_y(n, q, pair):
                    b = batch_of(nc, pair)
                    until(dve, z2_done, n + 1)
                    until(dve, y_stored[q], (n >> 1) * 16)
                    dve.tensor_tensor(y[:, q], ps[:, Y_BANK:Y_BANK + TT, 0:D],
                                      gates[:, 1, bass.ds(b, 1), :].broadcast_to((P, TT, D)),
                                      ALU.mult).then_inc(y_gated, 1)

                def result(n, q, pair):
                    b = batch_of(nc, pair)
                    until(dve, y_psum, n + 1)
                    link(dve.tensor_tensor(y_low[:], ps[:, Y_BANK:Y_BANK + TT, 0:D],
                                           gates[:, 1, bass.ds(b, 1), :].broadcast_to((P, TT, D)), ALU.mult))
                    until(dve, y_based, n + 1)
                    dve.tensor_tensor(y[:, q], y[:, q], y_low[:], ALU.add).then_inc(y_done, 1)

                def step(n, q, nb, fb, back, front):
                    base[0], made[0] = n * (FRONT + REST) + (FRONT - REST if back else FRONT), 0
                    pair = nb if q == 1 else nb - 1
                    if back:
                        route_hidden(n - 1)
                        gate_y(n - 1, 1 - q, pair)
                    if front:
                        low_o(n + 1, 1 - q)
                    for m in range(4):
                        hid_low(n, m)
                    if back:
                        result(n - 1, 1 - q, pair)
                    if front:
                        residual(n + 1, 1 - q, fb)
                    hid_low(n, 4)
                    hid_low(n, 5)
                    if front:
                        standardise_x1(n + 1, 1 - q)
                    hid_low(n, 6)
                    hid_low(n, 7)
                    if front:
                        low(n + 1, 1 - q)
                        route_in(n + 1)

                dve.memset(eps[:], EPS).then_inc(ready4, 1)
                dve.memset(zg[:], 0.0).then_inc(ready4, 1)
                invert(dve, NG - 1, 1)
                dve.wait_ge(ready4, 2)
                low_o(0, 0)
                residual(0, 0, 0)
                standardise_x1(0, 0)
                low(0, 0)
                route_in(0)
                by_steps(step)(dve)
                base[0], made[0] = NBLK * FRONT + (NBLK - 1) * REST, 0
                route_hidden(NBLK - 1)
                gate_y(NBLK - 1, 1, NBLK // 2 - 1)
                result(NBLK - 1, 1, NBLK // 2 - 1)


_NAMES = ["x", "cT", "wmod", "wqkvT", "bqkv", "bv", "woutT", "bout", "w1", "b1", "ar1", "bl1", "w2", "b2",
          "ar2", "bl2"]


def kernel(**inputs):
    import numpy as np
    import concourse.bacc as bacc
    from concourse.bass_utils import run_bass_kernel_spmd

    a = {k.removeprefix("L0_"): np.asarray(v) for k, v in inputs.items()}
    laid = {
        "x": a["attn_x"].reshape(T, D), "cT": a["c"].T, "wmod": a["wmod"],
        "wqkvT": a["attn_W_qkv"].T, "bqkv": a["attn_b_qkv"][:2 * D].reshape(2 * KC, P).T,
        "bv": a["attn_b_qkv"][2 * D:].reshape(1, D), "woutT": a["attn_W_out"].T,
        "bout": a["attn_b_out"].reshape(1, D), "w1": a["ffn_W1"], "b1": a["ffn_b1"].reshape(FC, P).T,
        "ar1": np.concatenate([a["ffn_A1"].transpose(1, 0, 2).reshape(D, ER), a["ffn_R1"]], 1),
        "bl1": a["ffn_B1"].reshape(ER, FF), "w2": a["ffn_W2"], "b2": a["ffn_b2"].reshape(1, D),
        "ar2": np.concatenate([a["ffn_A2"].transpose(1, 0, 2).reshape(FF, ER), a["ffn_R2"]], 1),
        "bl2": a["ffn_B2"].reshape(ER, D),
    }
    nc = bacc.Bacc("TRN2", target_bir_lowering=False, num_devices=1)
    arrays, args = {}, []
    for name in _NAMES:
        arr = np.ascontiguousarray(laid[name])
        arrays[f"in_{name}"] = arr
        args.append(nc.dram_tensor(f"in_{name}", arr.shape, mybir.dt.from_np(arr.dtype), kind="ExternalInput").ap())
    args.append(nc.dram_tensor("out", (T, D), F32, kind="ExternalOutput").ap())
    build_program(nc, *args)
    r = run_bass_kernel_spmd(nc, [arrays], core_ids=[0])
    return r.results[0]["out"].reshape(B, S, D)
```
